# Optimizing a Trainium2 kernel written in Bass

```python
import numpy as np
import jax
import jax.numpy as jnp

def _softmax(x, axis=-1):
    return jax.nn.softmax(x, axis=axis)

def _gelu(x):
    return jax.nn.gelu(x, approximate=True)

def _silu(x):
    return jax.nn.silu(x)

def _sigmoid(x):
    return jax.nn.sigmoid(x)

def _layernorm(x, axis=-1, eps=1e-05):
    m = jnp.mean(x, axis=axis, keepdims=True)
    v = jnp.var(x, axis=axis, keepdims=True)
    return (x - m) / jnp.sqrt(v + eps)

def _scatter_add(tgt, idx, src, axis=0):
    return tgt.at[idx].add(src)

def _segment_sum(src, seg, n):
    return jax.ops.segment_sum(src, seg, n)
kernel_name = 'mk_decoder_postln_d1_seqx_r4_3ab89f'

def setup_inputs(seed: int=0):
    np.random.seed(seed)
    _w = jnp.asarray

    def _rec_inputs():
        import jax
        import jax.numpy as jnp
        _rk = jax.random.key(seed)
        x = -0.0002928 + 1 * jax.random.normal(jax.random.fold_in(_rk, 1), (16, 256, 256), jnp.float32)
        _lenS = 256 - jax.random.randint(jax.random.fold_in(_rk, 7), (16,), 0, max(1, 256 // 4) + 1, jnp.int32)
        _lenS2 = 256 - jax.random.randint(jax.random.fold_in(_rk, 8), (16,), 0, max(1, 256 // 4) + 1, jnp.int32)
        _ctx_1024P = jax.random.normal(jax.random.fold_in(_rk, 11), (16, 16, 256), jnp.float32)
        _ctx_1024c = jax.random.dirichlet(jax.random.fold_in(_rk, 511), 0.3 * jnp.ones((16,), jnp.float32), (16, 256))
        _ctx_1024t = jnp.einsum('bsk,bkd->bsd', _ctx_1024c, _ctx_1024P)
        _ctx_1024t = _ctx_1024t * jax.lax.rsqrt(jnp.mean(jnp.square(_ctx_1024t)) + 1e-12) * 0.953939
        ctx_1024 = -1.39393e-06 + 0.999914 * (_ctx_1024t + 0.3 * jax.random.normal(jax.random.fold_in(_rk, 611), (16, 256, 256), jnp.float32))
        fside_BxS2_0 = jax.random.uniform(jax.random.fold_in(_rk, 12), (16, 256), jnp.float32, 0.0, 0.999833)
        return (x, ctx_1024, fside_BxS2_0)
    x, ctx_1024, fside_BxS2_0 = _rec_inputs()

    def _L0_attn_setup():
        import jax, jax.numpy as jnp
        import numpy as np
        B, T, C = (4, 512, 256)
        QH = 4
        D = C // QH
        EPS = 1e-05

        def _layernorm(x, g, b):
            mu = jnp.mean(x, axis=-1, keepdims=True)
            var = jnp.mean(jnp.square(x - mu), axis=-1, keepdims=True)
            return (x - mu) * jax.lax.rsqrt(var + EPS) * g + b
        key = jax.random.key(seed)
        k1, k2, k3 = jax.random.split(key, 3)
        residual = jax.random.normal(k1, (B, T, C), dtype=jnp.float32)
        w_fc = jax.random.normal(k2, (C, C), dtype=jnp.float32) * (1.0 / np.sqrt(C))
        w_proj = jax.random.normal(k3, (C, C), dtype=jnp.float32) * (1.0 / np.sqrt(C))
        ln_g = jnp.ones((C,), dtype=jnp.float32)
        ln_b = jnp.zeros((C,), dtype=jnp.float32)
        return {'residual': residual, 'w_fc': w_fc, 'w_proj': w_proj, 'ln_g': ln_g, 'ln_b': ln_b}
    _L0_attn_all = _L0_attn_setup()
    _L0_attn_in = {k: v for k, v in _L0_attn_all.items() if k in ('w_fc', 'w_proj', 'ln_g', 'ln_b')}
    del _L0_attn_all

    def _L0_xattn_setup():
        import jax, jax.numpy as jnp
        import numpy as np
        D_MODEL = 256
        NHEAD = 16
        HEAD_DIM = D_MODEL // NHEAD
        CLAMP_MIN = -0.2
        CLAMP_MAX = 0.2
        key = jax.random.key(seed)
        ks = jax.random.split(key, 16)
        B, T = (2, 512)
        s = 1.0 / np.sqrt(D_MODEL)
        inp = {'query': jax.random.normal(ks[0], (B, T, D_MODEL), jnp.float32), 'key': jax.random.normal(ks[1], (B, T, D_MODEL), jnp.float32), 'value': jax.random.normal(ks[2], (B, T, D_MODEL), jnp.float32), 'frac': jax.random.uniform(ks[3], (B, T), jnp.float32), 'Wq': jax.random.normal(ks[4], (D_MODEL, D_MODEL), jnp.float32) * s, 'bq': jnp.zeros((D_MODEL,), jnp.float32), 'Wk': jax.random.normal(ks[5], (D_MODEL, D_MODEL), jnp.float32) * s, 'bk': jnp.zeros((D_MODEL,), jnp.float32), 'Wv': jax.random.normal(ks[6], (D_MODEL, D_MODEL), jnp.float32) * s, 'bv': jnp.zeros((D_MODEL,), jnp.float32), 'Wo': jax.random.normal(ks[7], (D_MODEL, D_MODEL), jnp.float32) * s, 'bo': jnp.zeros((D_MODEL,), jnp.float32), 'alpha_pos': jax.random.normal(ks[8], (NHEAD,), jnp.float32) * 0.1, 'alpha_neg': jax.random.normal(ks[9], (NHEAD,), jnp.float32) * 0.1, 'gamma': jnp.float32(1.0), 'delta': jnp.float32(1.0)}
        return inp
    _L0_xattn_all = _L0_xattn_setup()
    _L0_xattn_in = {k: v for k, v in _L0_xattn_all.items() if k in ('Wq', 'bq', 'Wk', 'bk', 'Wv', 'bv', 'Wo', 'bo', 'alpha_pos', 'alpha_neg', 'gamma', 'delta')}
    del _L0_xattn_all

    def _L0_ffn_setup():
        import jax, jax.numpy as jnp
        import numpy as np
        B, S, D, F, E, R = (4, 512, 256, 1024, 8, 4)
        key = jax.random.key(seed)
        ks = jax.random.split(key, 8)
        s_in = 1.0 / np.sqrt(D)
        s_ff = 1.0 / np.sqrt(F)
        return {'hidden_states': jax.random.normal(ks[0], (B, S, D), jnp.float32), 'gate_W': jax.random.normal(ks[1], (E, D), jnp.float32) * s_in, 'gate_b': jnp.zeros((E,), jnp.float32), 'wi_W': jax.random.normal(ks[2], (F, D), jnp.float32) * s_in, 'wi_b': jnp.zeros((F,), jnp.float32), 'wo_W': jax.random.normal(ks[3], (D, F), jnp.float32) * s_ff, 'wo_b': jnp.zeros((D,), jnp.float32), 'lora_A': jax.random.normal(ks[4], (E, R, D), jnp.float32) * s_in, 'lora_B': jax.random.normal(ks[5], (E, F, R), jnp.float32) * 0.02}
    _L0_ffn_all = _L0_ffn_setup()
    _L0_ffn_in = {k: v for k, v in _L0_ffn_all.items() if k in ('gate_W', 'gate_b', 'wi_W', 'wi_b', 'wo_W', 'wo_b', 'lora_A', 'lora_B')}
    del _L0_ffn_all
    return {'x': x, 'ctx_1024': ctx_1024, 'fside_BxS2_0': fside_BxS2_0, 'L0_attn_w_fc': _L0_attn_in['w_fc'], 'L0_attn_w_proj': _L0_attn_in['w_proj'], 'L0_attn_ln_g': _L0_attn_in['ln_g'], 'L0_attn_ln_b': _L0_attn_in['ln_b'], 'L0_xattn_Wq': _L0_xattn_in['Wq'], 'L0_xattn_bq': _L0_xattn_in['bq'], 'L0_xattn_Wk': _L0_xattn_in['Wk'], 'L0_xattn_bk': _L0_xattn_in['bk'], 'L0_xattn_Wv': _L0_xattn_in['Wv'], 'L0_xattn_bv': _L0_xattn_in['bv'], 'L0_xattn_Wo': _L0_xattn_in['Wo'], 'L0_xattn_bo': _L0_xattn_in['bo'], 'L0_xattn_alpha_pos': _L0_xattn_in['alpha_pos'], 'L0_xattn_alpha_neg': _L0_xattn_in['alpha_neg'], 'L0_xattn_gamma': _L0_xattn_in['gamma'], 'L0_xattn_delta': _L0_xattn_in['delta'], 'L0_ffn_gate_W': _L0_ffn_in['gate_W'], 'L0_ffn_gate_b': _L0_ffn_in['gate_b'], 'L0_ffn_wi_W': _L0_ffn_in['wi_W'], 'L0_ffn_wi_b': _L0_ffn_in['wi_b'], 'L0_ffn_wo_W': _L0_ffn_in['wo_W'], 'L0_ffn_wo_b': _L0_ffn_in['wo_b'], 'L0_ffn_lora_A': _L0_ffn_in['lora_A'], 'L0_ffn_lora_B': _L0_ffn_in['lora_B']}

def reference(x, ctx_1024, fside_BxS2_0, L0_attn_w_fc, L0_attn_w_proj, L0_attn_ln_g, L0_attn_ln_b, L0_xattn_Wq, L0_xattn_bq, L0_xattn_Wk, L0_xattn_bk, L0_xattn_Wv, L0_xattn_bv, L0_xattn_Wo, L0_xattn_bo, L0_xattn_alpha_pos, L0_xattn_alpha_neg, L0_xattn_gamma, L0_xattn_delta, L0_ffn_gate_W, L0_ffn_gate_b, L0_ffn_wi_W, L0_ffn_wi_b, L0_ffn_wo_W, L0_ffn_wo_b, L0_ffn_lora_A, L0_ffn_lora_B):
    import jax
    import jax.numpy as jnp

    def _L0_attn_ref(residual, w_fc, w_proj, ln_g, ln_b):
        import jax, jax.numpy as jnp
        import numpy as np
        B, T, C = (4, 512, 256)
        QH = 4
        D = C // QH
        EPS = 1e-05

        def _layernorm(x, g, b):
            mu = jnp.mean(x, axis=-1, keepdims=True)
            var = jnp.mean(jnp.square(x - mu), axis=-1, keepdims=True)
            return (x - mu) * jax.lax.rsqrt(var + EPS) * g + b
        Bx, Tx, Cx = residual.shape
        x = _layernorm(residual, ln_g, ln_b)
        q = x.reshape(Bx, Tx, QH, D).transpose(0, 2, 1, 3)
        k = w_fc.reshape(-1, D)
        v = w_proj.T.reshape(-1, D)
        scores = jnp.einsum('bhtd,sd->bhts', q, k)
        p = jnp.square(jax.nn.relu(scores))
        out = jnp.einsum('bhts,sd->bhtd', p, v)
        out = out.transpose(0, 2, 1, 3).reshape(Bx, Tx, Cx)
        return residual + out

    def _L0_xattn_ref(query, key, value, frac, Wq, bq, Wk, bk, Wv, bv, Wo, bo, alpha_pos, alpha_neg, gamma, delta):
        import jax, jax.numpy as jnp
        import numpy as np
        D_MODEL = 256
        NHEAD = 16
        HEAD_DIM = D_MODEL // NHEAD
        CLAMP_MIN = -0.2
        CLAMP_MAX = 0.2
        B, T, _ = query.shape
        scale = HEAD_DIM ** (-0.5)

        def proj(x, W, b):
            y = x @ W.T + b
            return y.reshape(B, T, NHEAD, HEAD_DIM).transpose(0, 2, 1, 3)
        Q = proj(query, Wq, bq)
        K = proj(key, Wk, bk)
        V = proj(value, Wv, bv)
        logits = jnp.einsum('bhqd,bhkd->bhqk', Q, K) * scale
        D = jnp.clip(frac[:, None, :] - frac[:, :, None], CLAMP_MIN, CLAMP_MAX)
        D_pos = jnp.maximum(D, 0.0)
        D_neg = jnp.minimum(D, 0.0)
        ap = alpha_pos[None, :, None, None]
        an = alpha_neg[None, :, None, None]
        stoich_bias = ap * D_pos[:, None] + an * D_neg[:, None]
        attn = gamma * logits + delta * stoich_bias
        probs = jax.nn.softmax(attn, axis=-1)
        out = jnp.einsum('bhqk,bhkd->bhqd', probs, V)
        out = out.transpose(0, 2, 1, 3).reshape(B, T, D_MODEL)
        return out @ Wo.T + bo

    def _L0_ffn_ref(hidden_states, gate_W, gate_b, wi_W, wi_b, wo_W, wo_b, lora_A, lora_B):
        import jax, jax.numpy as jnp
        import numpy as np
        B, S, D, F, E, R = (4, 512, 256, 1024, 8, 4)
        x = hidden_states
        logits = jnp.einsum('bsd,ed->bse', x, gate_W) + gate_b
        top1 = jnp.argmax(jax.nn.softmax(logits, axis=-1), axis=-1)
        base = jnp.einsum('bsd,fd->bsf', x, wi_W) + wi_b
        out = jnp.zeros_like(x)
        for i in range(lora_A.shape[0]):
            lora = jnp.einsum('bsr,fr->bsf', jnp.einsum('bsd,rd->bsr', x, lora_A[i]), lora_B[i])
            inter = jax.nn.relu(base + lora)
            expert_out = jnp.einsum('bsf,df->bsd', inter, wo_W) + wo_b
            mask = (top1 == i).astype(x.dtype)[..., None]
            out = out + mask * expert_out
        return out
    x = _layernorm(x + _L0_attn_ref(x, L0_attn_w_fc, L0_attn_w_proj, L0_attn_ln_g, L0_attn_ln_b), axis=-1)
    x = _layernorm(x + _L0_xattn_ref(x, ctx_1024, ctx_1024, fside_BxS2_0, L0_xattn_Wq, L0_xattn_bq, L0_xattn_Wk, L0_xattn_bk, L0_xattn_Wv, L0_xattn_bv, L0_xattn_Wo, L0_xattn_bo, L0_xattn_alpha_pos, L0_xattn_alpha_neg, L0_xattn_gamma, L0_xattn_delta), axis=-1)
    x = _layernorm(x + _L0_ffn_ref(x, L0_ffn_gate_W, L0_ffn_gate_b, L0_ffn_wi_W, L0_ffn_wi_b, L0_ffn_wo_W, L0_ffn_wo_b, L0_ffn_lora_A, L0_ffn_lora_B), axis=-1)
    return x

_drawn_inputs = setup_inputs


def setup_inputs(seed=0):
    import zlib

    import numpy as np

    out = dict(_drawn_inputs(seed))
    spreads = {'L0_attn_ln_g': (1.0, 0.2),
     'L0_attn_ln_b': (0.0, 0.1),
     'L0_xattn_bq': (0.0, 0.397),
     'L0_xattn_bk': (0.0, 2.0),
     'L0_xattn_bv': (0.0, 0.1),
     'L0_xattn_bo': (0.0, 0.1),
     'L0_ffn_gate_b': (0.0, 2.0),
     'L0_ffn_wi_b': (0.0, 0.1),
     'L0_ffn_wo_b': (0.0, 0.1)}
    factors = {'fside_BxS2_0': 58.873,
     'L0_xattn_alpha_pos': 64.0,
     'L0_xattn_alpha_neg': 64.0,
     'L0_ffn_gate_W': 9.352}
    for name, (base, spread) in spreads.items():
        noise = np.random.default_rng([zlib.crc32(name.encode()), seed]).standard_normal(out[name].shape)
        drawn = base * np.exp(spread * noise) if base else spread * noise
        out[name] = jnp.asarray(drawn.astype(out[name].dtype))
    for name, factor in factors.items():
        out[name] = (out[name] * factor).astype(out[name].dtype)
    return out
```

```python
import concourse.bass as bass
from concourse import mybir
from contextlib import ExitStack


def decoder_layer(nc, a, out):
    f32 = mybir.dt.float32
    f32r = mybir.dt.float32r
    ALU = mybir.AluOpType
    ACT = mybir.ActivationFunctionType
    AX = mybir.AxisListType

    NB = 16
    EPS = 1e-5
    CLIP = 0.2
    BIG = 3.0e38

    ctx = ExitStack()
    with ctx:
        def sb(name, shape, dt=f32):
            return ctx.enter_context(nc.sbuf_tensor(name, shape, dt))

        def sem(name):
            return ctx.enter_context(nc.semaphore(name))

        class Later:

            def activation(self, *a, **k):
                return lambda e: e.activation(*a, **k)

            def affine_select(self, *a, **k):
                return lambda e: e.affine_select(*a, **k)

            def bn_aggr(self, *a, **k):
                return lambda e: e.bn_aggr(*a, **k)

            def bn_stats(self, *a, **k):
                return lambda e: e.bn_stats(*a, **k)

            def dma_start(self, *a, **k):
                return lambda e: e.dma_start(*a, **k)

            def matmul(self, *a, **k):
                return lambda e: e.matmul(*a, **k)

            def memset(self, *a, **k):
                return lambda e: e.memset(*a, **k)

            def reciprocal(self, *a, **k):
                return lambda e: e.reciprocal(*a, **k)

            def scalar_tensor_tensor(self, *a, **k):
                return lambda e: e.scalar_tensor_tensor(*a, **k)

            def tensor_copy(self, *a, **k):
                return lambda e: e.tensor_copy(*a, **k)

            def tensor_reduce(self, *a, **k):
                return lambda e: e.tensor_reduce(*a, **k)

            def tensor_scalar(self, *a, **k):
                return lambda e: e.tensor_scalar(*a, **k)

            def tensor_tensor(self, *a, **k):
                return lambda e: e.tensor_tensor(*a, **k)

            def tensor_tensor_reduce(self, *a, **k):
                return lambda e: e.tensor_tensor_reduce(*a, **k)

            def transpose(self, *a, **k):
                return lambda e: e.transpose(*a, **k)

        later = Later()

        class Lane:

            def __init__(self, name):
                self.name, self.sem, self.n, self.queue, self.seen = name, sem("s_" + name), 0, [], {}

            def wait(self, *tokens):
                for t in tokens:
                    if type(t) is list:
                        self.wait(*t)
                    elif t is not None and self.seen.get(t[0].name, 0) < t[1]:
                        self.seen[t[0].name] = t[1]
                        self.queue.append((t[0], t[1], None))

            def do(self, fn, *tokens, signal=True):
                self.wait(*tokens)
                fn = fn(later)
                if not signal:
                    self.queue.append((None, 0, fn))
                    return None
                self.n += 1
                self.queue.append((self.sem, 1, fn))
                return (self.sem, self.n)

            def run(self, eng):
                for s, v, fn in self.queue:
                    if fn is None:
                        eng.wait_ge(s, v)
                    elif s is None:
                        fn(eng)
                    else:
                        fn(eng).then_inc(s, v)

        PE, ACTE, DVE, POOL, SP = (Lane(n) for n in ("pe", "act", "dve", "pool", "sp"))

        class Stream:

            def __init__(self, name):
                self.sem, self.n = sem("d_" + name), 0

            def dma(self, dst, src, *tokens):
                SP.wait(*tokens)
                if src.dtype == f32r:
                    dst, src = dst.bitcast(f32), src.bitcast(f32)
                self.n += 16
                SP.queue.append((self.sem, 16, lambda e: e.dma_start(dst, src)))
                return (self.sem, self.n)

        psum = [ctx.enter_context(nc.psum_tensor(f"bank{i}", [128, 512], f32)) for i in range(8)]
        pL, pT, pV, pA = psum[3:5], psum[5], psum[6], psum[7]

        class Banks:

            def __init__(self):
                self.free = [(psum[i], None) for i in range(3)]

            def get(self):
                return self.free.pop(0)

            def put(self, bank, token):
                self.free.append((bank, token))

        M = Banks()

        def rel(bank, token):
            M.put(bank, token)

        ident = sb("ident", [128, 128])
        KH, KL = sb("KH", [128, 1024], f32r), sb("KL", [128, 1024], f32r)
        VS = sb("VS", [128, 8, 64])
        W = {}
        for n in ("q", "k", "v", "o"):
            W[n] = (sb(f"W{n}h", [128, 2, 256], f32r), sb(f"W{n}l", [128, 2, 256], f32r))
        WI = (sb("WIh", [128, 2, 1024], f32r), sb("WIl", [128, 2, 1024], f32r))
        WP = (sb("WPh", [128, 8, 256], f32r), sb("WPl", [128, 8, 256], f32r))
        GA = (sb("GAh", [128, 2, 40], f32r), sb("GAl", [128, 2, 40], f32r))
        LB = sb("LB", [128, 1024], f32r)
        gB, bB = sb("gB", [128, 256]), sb("bB", [128, 256])
        boB, woB = sb("boB", [128, 256]), sb("woB", [128, 256])
        bqk = sb("bqk", [128, 4])
        bvc = sb("bvc", [128, 2])
        gate_b = sb("gate_b", [40, 1])
        fT = sb("fT", [128, 32])
        alph = sb("alph", [128, 32])
        gd = sb("gd", [128, 2])
        mhalf = sb("mhalf", [128, 2])
        dec8 = sb("dec8", [128, 8])

        NX = 2
        XG = [sb(f"XG{i}", [128, 2, 256]) for i in range(NX)]
        XN = sb("XN", [128, 2, 256])
        SK = sb("SK", [128, 2, 2, 256], f32r)
        NR = 6
        R = [sb(f"R{i}", [128, 512]) for i in range(NR)]
        OT = sb("OT", [128, 2, 256])
        X1 = sb("X1", [128, 2, 256])
        X1b = sb("X1b", [128, 2, 256])
        X1H, X1L = sb("X1H", [128, 2, 256], f32r), sb("X1L", [128, 2, 256], f32r)
        CT = [sb(f"CT{i}", [128, 2, 256]) for i in range(2)]
        CH, CL = sb("CH", [128, 2, 256], f32r), sb("CL", [128, 2, 256], f32r)
        QK = {n: sb(n, [128, 2, 256], f32r) for n in ("QH", "QL", "KKH", "KKL")}
        NS = 2
        QS = [sb(f"QS{i}", [128, 4, 256], f32r) for i in range(NS)]
        KS = [sb(f"KS{i}", [128, 4, 256], f32r) for i in range(NS)]
        vv = sb("VV", [128, 2, 16, 32])
        FK = sb("FK", [128, 256])
        dp, dn = sb("DP", [128, 512]), sb("DN", [128, 512])
        NU, NT, NP, NQ = 2, 3, 2, 6
        U = [sb(f"U{i}", [128, 512]) for i in range(NU)]
        T = [sb(f"T{i}", [128, 512]) for i in range(NT)]
        NM = sb("NM", [128, 8, 2])
        P = [sb(f"P{i}", [128, 512]) for i in range(NP)]
        STG = sb("STG", [128, NQ, 512])
        PT = [STG[:, i, :] for i in range(NQ)]
        OV = [sb(f"OV{i}", [128, 2, 256]) for i in range(2)]
        RC = sb("RC", [128, 2, 16])
        AO = sb("AO", [128, 2, 256])
        X2 = sb("X2", [128, 2, 256])
        X2b = sb("X2b", [128, 2, 256])
        X2H, X2L = sb("X2H", [128, 2, 256], f32r), sb("X2L", [128, 2, 256], f32r)
        GS = sb("GS", [40, 256])
        g1, g2 = sb("g1", [128, 2, 8]), sb("g2", [128, 2, 8])
        gm = sb("gm", [128, 4])
        U2 = sb("U2", [128, 2, 32])
        UL = sb("UL", [128, 256], f32r)
        IH, IL = sb("IH", [128, 4, 512], f32r), sb("IL", [128, 4, 512], f32r)
        XO = [sb(f"XO{i}", [128, 2, 256]) for i in range(2)]
        SM = {k: sb("SM" + k, [128, 24]) for k in "abcd"}

        def f(ap):
            return ap.bitcast(f32)

        def split(hi, lo, src, src_tok, hi_free, lo_free):
            th = ACTE.do(lambda e: e.activation(hi, src, ACT.Copy), src_tok, hi_free)
            tl = DVE.do(lambda e: e.tensor_tensor(lo, src, f(hi), ALU.subtract), th, src_tok, lo_free)
            return th, tl

        def normalise(dst, src, src_tok, dst_free, k):
            s = SM[k]
            st = s[:, 0:12].rearrange("p (t c) -> p t c", t=2)
            mv = s[:, 12:16].rearrange("p (t c) -> p t c", t=2)
            for t in range(2):
                tk = DVE.do(lambda e, t=t: e.bn_stats(st[:, t, :], src[:, t, :]), src_tok)
            for t in range(2):
                tk = DVE.do(lambda e, t=t: e.bn_aggr(mv[:, t, :], st[:, t, :]), tk)
            tk = DVE.do(lambda e: e.tensor_scalar(s[:, 16:18], mv[:, :, 1], EPS, None, ALU.add), tk)
            tk = POOL.do(lambda e: e.tensor_tensor(s[:, 18:20], s[:, 16:18], mhalf[:, :], ALU.pow), tk)
            for t in range(2):
                last = DVE.do(lambda e, t=t: e.tensor_scalar(dst[:, t, :], src[:, t, :], mv[:, t, 0:1],
                                                             s[:, 18 + t:19 + t], ALU.subtract, ALU.mult),
                              tk, dst_free)
            return last

        def transposed(src, src_tok, hi, lo, hi_free, lo_free):
            while not M.free:
                yield
            bank, free = M.get()
            for m in range(2):
                for t in range(2):
                    tk = PE.do(lambda e, m=m, t=t: e.transpose(
                        bank[:, m * 256 + t * 128:m * 256 + t * 128 + 128],
                        src[:, t, m * 128:m * 128 + 128], ident[:, :]), src_tok, free, signal=(m + t == 2))
            b3 = bank[:, :].rearrange("p (m t) -> p m t", m=2)
            th, tl = split(hi, lo, b3, tk, hi_free, lo_free)
            rel(bank, tl)
            return th, tl

        def mm3(bank_ap, pairs, tokens, signal):
            n = len(pairs)
            tk = None
            for i, (lh, ll, rh, rl) in enumerate(pairs):
                for j, (x, y) in enumerate(((lh, rh), (lh, rl), (ll, rh))):
                    s, e_ = (i == 0 and j == 0), (i == n - 1 and j == 2)
                    tk = PE.do(lambda e, x=x, y=y, s=s, e_=e_: e.matmul(bank_ap, x, y, start=s, stop=e_),
                               *tokens, signal=signal and e_)
            return tk

        last = {}

        dS = Stream("small")
        tok_small = None
        for dst, src in ((gB, a["ln_g"]), (bB, a["ln_b"]), (boB, a["bo"]), (woB, a["wo_b"])):
            tok_small = dS.dma(dst[:, :], src.partition_broadcast(128))
        tok_small = dS.dma(alph[:, 0:16], a["alpha_pos"].partition_broadcast(128))
        tok_small = dS.dma(alph[:, 16:32], a["alpha_neg"].partition_broadcast(128))
        tok_small = dS.dma(gd[:, 0:1], a["gamma"].partition_broadcast(128))
        tok_small = dS.dma(gd[:, 1:2], a["delta"].partition_broadcast(128))
        tok_small = dS.dma(bqk[:, 0:2], a["bq"])
        tok_small = dS.dma(bqk[:, 2:4], a["bk"])
        tok_small = dS.dma(bvc[:, :], a["bv"])
        tok_small = dS.dma(fT[:, :], a["fT"])
        tok_small = dS.dma(VS[:, :, :], a["v"].rearrange("(c p) d -> p c d", p=128))

        tk = POOL.do(lambda e: e.memset(ident[:, :], 0.0))
        tok_id = POOL.do(lambda e: e.affine_select(out=ident[:, :], in_=ident[:, :], compare_op=ALU.not_equal,
                                                   fill=1.0, base=0, pattern=[[-1, 128]],
                                                   channel_multiplier=1), tk)
        tok_mh = POOL.do(lambda e: e.memset(mhalf[:, :], -0.5))
        POOL.do(lambda e: e.memset(gate_b[:, :], 0.0))
        for i in range(8):
            tok_c = POOL.do(lambda e, i=i: e.memset(dec8[:, i:i + 1], float(8 - i)))
        tok_c = POOL.do(lambda e: e.memset(f(UL[96:128, :]), 1.0), tok_c)
        tok_lbz = POOL.do(lambda e: e.memset(f(LB[96:128, :]), 0.0), tok_c)
        tok_c = POOL.do(lambda e: e.memset(vv[:, :, :, 16:32], 0.0), tok_lbz)
        tok_c = POOL.do(lambda e: e.memset(vv[:, :, :, 16:17], 1.0), tok_c)
        for t in QS + KS:
            tok_zero = POOL.do(lambda e, t=t: e.memset(f(t[:, :, :]), 0.0))

        dX, dC, dF = [Stream(f"x{i}") for i in range(NX)], [Stream(f"c{i}") for i in range(2)], Stream("f")

        def load_x(b, free):
            return dX[b % NX].dma(XG[b % NX][:, :, :],
                                 a["x"][b * 256:b * 256 + 256, :].rearrange("(t p) c -> p t c", p=128), free)

        def load_c(b, free):
            return dC[b % 2].dma(CT[b % 2][:, :, :],
                                 a["ctxT"][:, b * 256:b * 256 + 256].rearrange("(k p) t -> p k t", p=128), free)

        def load_f(b, free):
            return dF.dma(FK[:, :], a["frac"][b, :].partition_broadcast(128), free)

        xl, cl, fl = {0: load_x(0, None)}, {}, {}

        def stage(n_cols, slot):
            return STG[:, slot:slot + (n_cols + 511) // 512, :].rearrange("p a b -> p (a b)")[:, 0:n_cols]

        dW = [Stream(f"w{i}") for i in range(3)]
        reg = [(0, 2), (2, 2), (4, 2)]
        jobs = []
        free = [None, None, None]

        def weight(i, src_ap, parts, shape, hi, lo, scale=None, scale_tok=None):
            st = stage(shape[0] * shape[1], reg[i][0])[0:parts, :]
            v = st.rearrange("p (a b) -> p a b", a=shape[0])
            tk = dW[i].dma(v, src_ap, free[i])
            if scale is not None:
                tk = DVE.do(lambda e: e.tensor_scalar(v, v, scale[0:parts, :], 0.25, ALU.mult, ALU.mult),
                            tk, scale_tok)
            th, tl = split(hi, lo, v, tk, None, None)
            free[i] = tl
            return tl

        st = stage(1024, 0)
        dW[0].dma(st[0:64, :], a["kT"])
        tk = dW[0].dma(st[64:128, :], a["kT"])
        tok_kh, tok_k = split(KH[:, :], KL[:, :], st, tk, None, None)
        free[0] = tok_k

        def col(src, k):
            return src.rearrange("(k p) e -> p k e", p=128)

        tok_w = {}

        def weights():
            nonlocal tok_small, tok_c
            t1 = DVE.do(lambda e: e.tensor_scalar(bqk[:, 0:2], bqk[:, 0:2], gd[:, 0:1], 0.25, ALU.mult, ALU.mult),
                        (dS.sem, dS.n))
            t2 = DVE.do(lambda e: e.tensor_scalar(alph[:, :], alph[:, :], gd[:, 1:2], None, ALU.mult))
            tok_w["small"] = t2
            tok_w["v"] = weight(1, col(a["WvT"], 2), 128, (2, 256), W["v"][0][:, :, :], W["v"][1][:, :, :])
            yield
            tok_w["k"] = weight(2, col(a["WkT"], 2), 128, (2, 256), W["k"][0][:, :, :], W["k"][1][:, :, :])
            yield
            tok_w["q"] = weight(0, col(a["WqT"], 2), 128, (2, 256), W["q"][0][:, :, :], W["q"][1][:, :, :],
                                gd[:, 0:1], (dS.sem, dS.n))
            yield
            st = stage(512, reg[1][0])
            v = st.rearrange("p (a b) -> p a b", a=2)
            tk = dW[1].dma(v, col(a["WoT"], 2), free[1])
            th, tl = split(W["o"][0][:, :, :], W["o"][1][:, :, :], v, tk, None, None)
            while not M.free:
                yield
            bank, bf = M.get()
            for k in range(2):
                tp = PE.do(lambda e, k=k: e.matmul(bank[:, 0:256], bvc[:, k:k + 1].to_broadcast([128, 128]),
                                                   v[:, k, :], start=(k == 0), stop=(k == 1)),
                           bf, tk, (dS.sem, dS.n), signal=(k == 1))
            t3 = DVE.do(lambda e: e.tensor_tensor(boB[:, :], boB[:, :], bank[:, 0:256], ALU.add), tp)
            rel(bank, t3)
            free[1] = t3
            tok_w["o"] = t3
            yield
            for h in range(2):
                tok_w["i"] = weight(2 * h, a["wiT"][h * 128:h * 128 + 128, :].rearrange("p (a e) -> p a e", a=1),
                                    128, (1, 1024), WI[0][:, h:h + 1, :], WI[1][:, h:h + 1, :])
                yield
            for h in range(2):
                tok_w["p"] = weight(1 + h, a["woT"][h * 512:h * 512 + 512, :].rearrange("(k p) e -> p k e", p=128),
                                    128, (4, 256), WP[0][:, 4 * h:4 * h + 4, :], WP[1][:, 4 * h:4 * h + 4, :])
                yield
            st = stage(80, reg[0][0])
            v = st.rearrange("p (a b) -> p a b", a=2)
            dW[0].dma(v[:, :, 0:32], col(a["loraA"], 2), free[0])
            tk = dW[0].dma(v[:, :, 32:40], col(a["gateT"], 2))
            th, tl = split(GA[0][:, :, :], GA[1][:, :, :], v, tk, None, None)
            free[0] = tl
            tok_w["g"] = dS.dma(gate_b[32:40, :], a["gate_b"], tok_c)
            yield
            st = stage(1024, reg[1][0])
            for r in range(3):
                tk = dW[1].dma(st[32 * r:32 * r + 32, :], a["loraB"], free[1])
            th = ACTE.do(lambda e: e.activation(LB[0:96, :], st[0:96, :], ACT.Copy), tk)
            tl = DVE.do(lambda e: e.tensor_tensor(LB[64:96, :], st[64:96, :], f(LB[64:96, :]), ALU.subtract), th)
            bh, bl = IH[0:1, 0:2, :], IL[0:1, 0:2, :]
            st2 = stage(1024, reg[2][0])[0:1, :].rearrange("p (a b) -> p a b", a=2)
            tk = dW[2].dma(st2, a["wi_b"].rearrange("(o a b) -> o a b", o=1, a=2), free[2])
            th2, tl2 = split(bh, bl, st2, tk, None, None)
            t4 = dW[1].dma(LB[96:97, :].rearrange("p (a b) -> p a b", a=2), bh, th2, tl2, tok_lbz)
            t4 = dW[1].dma(LB[97:98, :].rearrange("p (a b) -> p a b", a=2), bl)
            tok_w["lb"] = (th, tl, t4)
            free[1] = free[2] = tl
            tok_w["stage"] = [tl, tl2, tok_w["g"]]
            yield

        x1_tok, x1t_tok = {}, {}

        def stage1(b):
            xg = XG[b % NX]
            if b + 1 < NB:
                xl[b + 1] = load_x(b + 1, last.get(("y1", b + 1 - NX)))
            if b == 0:
                cl[0], fl[0] = load_c(0, None), load_f(0, None)
            tx = normalise(XN, xg, xl[b], last.get("xn"), "a")
            gb = gB[:, :].unsqueeze(1).to_broadcast([128, 2, 256])
            bb = bB[:, :].unsqueeze(1).to_broadcast([128, 2, 256])
            tx = DVE.do(lambda e: e.tensor_tensor(XN[:, :, :], XN[:, :, :], gb, ALU.mult), tx, tok_small)
            tx = DVE.do(lambda e: e.tensor_tensor(XN[:, :, :], XN[:, :, :], bb, ALU.add), tx)
            yield
            while not M.free:
                yield
            bank, free_ = M.get()
            for hp in range(2):
                for t in range(2):
                    tk = PE.do(lambda e, hp=hp, t=t, bank=bank: e.transpose(
                        bank[:, hp * 256 + t * 128:hp * 256 + t * 128 + 128],
                        XN[:, t, hp * 128:hp * 128 + 128], ident[:, :]),
                        tx, free_, tok_id, signal=(hp + t == 2))
            last["xn"] = tk
            b3 = bank[:, :].rearrange("p (h t) -> p h t", h=2)
            for h in range(2):
                own, other = slice(64 * h, 64 * h + 64), slice(64 - 64 * h, 128 - 64 * h)
                th = ACTE.do(lambda e, h=h, own=own, b3=b3: e.activation(SK[own, :, h, :], b3[own, :, :], ACT.Copy),
                             tk, last.get("sk"))
                tl = DVE.do(lambda e, h=h, own=own, other=other, b3=b3: e.tensor_tensor(
                    SK[other, :, h, :], b3[own, :, :], f(SK[own, :, h, :]), ALU.subtract), th)
            rel(bank, tl)
            sk_tok = [th, tl]
            yield
            units = [(hp, c2, h) for hp in range(2) for c2 in range(4) for h in range(2)]
            sq = {}

            def av(j):
                hp, c2, _ = units[2 * j]
                for i in range(2):
                    for h in range(2):
                        r, ts = sq[2 * j + h]
                        c = 2 * c2 + i
                        tk = PE.do(lambda e, r=r, i=i, h=h, c=c, hp=hp: e.matmul(
                            pA[64 * h:64 * h + 64, hp * 256:hp * 256 + 256], VS[:, c, :],
                            r[:, i * 256:i * 256 + 256], start=(c == 0), stop=(c == 7),
                            skip_group_check=True),
                            ts, last.get("pA"), signal=(i == 1 and h == 1))
                for h in range(2):
                    last[("r", (last["rn"][2 * j + h]))] = tk
                return tk

            last["rn"] = {}
            for u, (hp, c2, h) in enumerate(units):
                while not M.free:
                    yield
                bank, free_ = M.get()
                for i in range(2):
                    c = 2 * c2 + i
                    for n, kk in enumerate((KH, KL)):
                        tk = PE.do(lambda e, bank=bank, i=i, c=c, kk=kk, n=n, hp=hp, h=h: e.matmul(
                            bank[:, i * 256:i * 256 + 256], kk[:, c * 128:c * 128 + 128], SK[:, hp, h, :],
                            start=(n == 0), stop=(n == 1)),
                            free_, sk_tok, tok_kh, tok_k, signal=(i == 1 and n == 1))
                last["sk"] = tk
                slot = (b * 16 + u) % NR
                r = R[slot]
                last["rn"][u] = slot
                tr = ACTE.do(lambda e, r=r, bank=bank: e.activation(r[:, :], bank[:, :], ACT.Relu), tk,
                             last.get(("r", slot)))
                rel(bank, tr)
                lane = DVE if u % 8 == 7 else POOL
                ts = lane.do(lambda e, r=r: e.tensor_tensor(r[:, :], r[:, :], r[:, :], ALU.mult), tr)
                sq[u] = (r, ts)
                if u % 2 == 1 and u >= 5:
                    av(u // 2 - 2)
                yield
            av(6)
            yield
            tk = av(7)
            to = ACTE.do(lambda e: e.activation(OT[:, :, :], pA[:, :].rearrange("p (h t) -> p h t", h=2),
                                                ACT.Copy), tk, last.get("ot"))
            last["pA"] = to
            yield
            while not M.free:
                yield
            bank, free_ = M.get()
            for t in range(2):
                for hp in range(2):
                    tk = PE.do(lambda e, t=t, hp=hp: e.transpose(
                        bank[:, t * 256 + hp * 128:t * 256 + hp * 128 + 128],
                        OT[:, hp, t * 128:t * 128 + 128], ident[:, :]), to, free_, signal=(t + hp == 2))
            last["ot"] = tk
            b3 = bank[:, :].rearrange("p (t c) -> p t c", t=2)
            ty = DVE.do(lambda e: e.scalar_tensor_tensor(out=xg[:, :, :], in0=xg[:, :, :], scalar=2.0, in1=b3,
                                                         op0=ALU.mult, op1=ALU.add), tk)
            rel(bank, ty)
            yield
            x1_tok[b] = normalise(X1, xg, ty, last.get("x1"), "b")
            last[("y1", b)] = x1_tok[b]
            yield

        dQ = [Stream(f"q{i}") for i in range(NS)]
        x2_tok = {}

        def stage2(b):
            if b + 1 < NB:
                cl[b + 1] = load_c(b + 1, last.get(("ct", b - 1)))
            ct = CT[b % 2]
            for q in range(2):
                td = DVE.do(lambda e, q=q: e.tensor_scalar(dn[:, q * 256:q * 256 + 256], FK[:, :],
                                                           fT[:, 2 * b + q:2 * b + q + 1], CLIP,
                                                           ALU.subtract, ALU.min), fl[b], last.get("d"))
            if b + 1 < NB:
                fl[b + 1] = load_f(b + 1, td)
            tdp = DVE.do(lambda e: e.tensor_scalar(dp[:, :], dn[:, :], 0.0, None, ALU.max), td)
            tdn = DVE.do(lambda e: e.tensor_scalar(dn[:, :], dn[:, :], -CLIP, 0.0, ALU.max, ALU.min), tdp)
            th, tl = split(CH[:, :, :], CL[:, :, :], ct[:, :, :], cl[b], last.get("ch"), last.get("ch"))
            last[("ct", b)] = tl
            yield
            xh, xlo = yield from transposed(X1, x1_tok[b], X1H[:, :, :], X1L[:, :, :],
                                            last.get("x1h"), last.get("x1h"))
            tx1b = POOL.do(lambda e: e.tensor_tensor(X1b[:, :, :], X1[:, :, :],
                                                     boB[:, :].unsqueeze(1).to_broadcast([128, 2, 256]), ALU.add),
                           x1_tok[b], tok_w["o"], last.get("x1b"))
            last["x1"] = [xh, tx1b]
            yield

            def project(n, src, toks, bias, hi, lo, key):
                while not M.free:
                    yield
                bank, free_ = M.get()
                wh, wl = W[n]
                for m in range(2):
                    cs = slice(m * 128, m * 128 + 128)
                    tk = mm3(bank[:, m * 256:m * 256 + 256],
                             [(wh[:, k, cs], wl[:, k, cs], src[0][:, k, :], src[1][:, k, :]) for k in range(2)],
                             [free_, tok_w[n], *toks], m == 1)
                for m in range(2):
                    bm = bank[:, m * 256:m * 256 + 256]
                    th = ACTE.do(lambda e, m=m, bm=bm: e.activation(hi[:, m, :], bm, ACT.Identity,
                                                                    bias=bqk[:, bias + m:bias + m + 1]),
                                 tk, last.get(key), tok_w["small"])
                for m in range(2):
                    bm = bank[:, m * 256:m * 256 + 256]
                    tl = DVE.do(lambda e, m=m, bm=bm: e.scalar_tensor_tensor(
                        out=lo[:, m, :], in0=bm, scalar=bqk[:, bias + m:bias + m + 1], in1=f(hi[:, m, :]),
                        op0=ALU.add, op1=ALU.subtract), th, last.get(key))
                rel(bank, tl)
                return th, tl, tk

            kt = yield from project("k", (CH, CL), (th, tl), 2, QK["KKH"], QK["KKL"], "qk")
            yield
            qt = yield from project("q", (X1H, X1L), (xh, xlo), 0, QK["QH"], QK["QL"], "qk")
            last["x1h"] = qt[2]
            yield
            made = (kt[0], kt[1], qt[0], qt[1])
            st_tok = {}

            def restack(g):
                n = b * 4 + g
                s, m, p0 = n % NS, g // 2, (g % 2) * 64
                d = dQ[s]
                for dst, parts in ((QS[s], ("QH", "QL", "QH")), (KS[s], ("KKH", "KKH", "KKL"))):
                    for r, part in enumerate(parts):
                        for j in range(4):
                            p = p0 + 16 * j
                            tk = d.dma(dst[16 * r:16 * r + 16, j, :], QK[part][p:p + 16, m, :],
                                       *made, last.get(("qs", s)), tok_zero)
                st_tok[g] = tk
                if g == 3:
                    last["qk"] = tk

            restack(0)
            while not M.free:
                yield
            bank, free_ = M.get()
            wh, wl = W["v"]
            for t in range(2):
                ts_ = slice(t * 128, t * 128 + 128)
                tk = mm3(bank[:, t * 256:t * 256 + 256],
                         [(CH[:, k, ts_], CL[:, k, ts_], wh[:, k, :], wl[:, k, :]) for k in range(2)],
                         [free_, tok_w["v"], th, tl], t == 1)
            last["ch"] = tk
            for t in range(2):
                tv = DVE.do(lambda e, t=t: e.tensor_copy(
                    vv[:, t, :, 0:16], bank[:, t * 256:t * 256 + 256].rearrange("p (h d) -> p h d", h=16)),
                    tk, last.get("vv"), tok_c)
            rel(bank, tv)
            restack(1)
            yield

            tlog, tu, texp, tev = {}, {}, {}, {}

            def logits(h):
                n = b * 16 + h
                s, L = (b * 4 + h // 4) % NS, pL[n % 2]
                for q in range(2):
                    tk = PE.do(lambda e, q=q: e.matmul(L[:, q * 256:q * 256 + 256],
                                                       QS[s][:, h % 4, q * 128:q * 128 + 128], KS[s][:, h % 4, :],
                                                       start=True, stop=True),
                               st_tok[h // 4], last.get(("L", n - 2)), signal=(q == 1))
                last[("qs", s)] = tk
                u = U[n % NU]
                tu = POOL.do(lambda e: e.tensor_scalar(u[:, :], dp[:, :], alph[:, h:h + 1], 0.0, ALU.mult, ALU.add),
                             tdp, last.get(("u", n - NU)), tok_w["small"])
                t = T[n % NT]
                t1 = DVE.do(lambda e: e.scalar_tensor_tensor(out=t[:, :], in0=dn[:, :],
                                                             scalar=alph[:, 16 + h:17 + h], in1=L[:, :],
                                                             op0=ALU.mult, op1=ALU.add),
                            tk, tdn, last.get(("t", n - NT)))
                last[("L", n)] = t1
                for q in range(2):
                    cs = slice(q * 256, q * 256 + 256)
                    t2 = DVE.do(lambda e, q=q, cs=cs: e.tensor_tensor_reduce(
                        out=t[:, cs], in0=t[:, cs], in1=u[:, cs], scale=-1.0, scalar=BIG, op0=ALU.add,
                        op1=ALU.min, accum_out=NM[:, n % 8, q:q + 1]), t1, tu, last.get(("t", n - 8)))
                last[("u", n)] = t2
                tlog[h] = t2

            def exps(h):
                n = b * 16 + h
                t, p = T[n % NT], P[n % NP]
                for q in range(2):
                    cs = slice(q * 256, q * 256 + 256)
                    tk = ACTE.do(lambda e, q=q, cs=cs: e.activation(p[:, cs], t[:, cs], ACT.Exp,
                                                                    bias=NM[:, n % 8, q:q + 1], scale=-1.0),
                                 tlog[h], last.get(("p", n - NP)))
                last[("t", n)] = tk
                texp[h] = tk

            def turn(h):
                n = b * 16 + h
                p, pt = P[n % NP], PT[n % NQ]
                for k in range(2):
                    for q in range(2):
                        tk = PE.do(lambda e, k=k, q=q: e.transpose(
                            pT[:, k * 256 + q * 128:k * 256 + q * 128 + 128],
                            p[:, q * 256 + k * 128:q * 256 + k * 128 + 128], ident[:, :]),
                            texp[h], last.get("pT"), signal=(k + q == 2))
                last[("p", n)] = tk
                extra = tok_w["stage"] if n < NQ else ()
                tev[h] = ACTE.do(lambda e: e.activation(pt, pT[:, :], ACT.Copy), tk, last.get(("pt", n - NQ)),
                                 *extra)
                last["pT"] = tev[h]

            def values(g):
                c0 = (g % 2) * 256
                for k in range(2):
                    for j in range(4):
                        h = 4 * g + j
                        pt = PT[(b * 16 + h) % NQ]
                        tk = PE.do(lambda e, k=k, j=j, h=h, pt=pt: e.matmul(
                            pV[32 * j:32 * j + 32, c0:c0 + 256], vv[:, k, h, :], pt[:, k * 256:k * 256 + 256],
                            start=(k == 0), stop=(k == 1), skip_group_check=True),
                            tev[h], tv, last.get("pV"), signal=(k == 1 and j == 3))
                for j in range(4):
                    last[("pt", b * 16 + 4 * g + j)] = tk
                if g % 2:
                    ov = OV[g // 2]
                    to = ACTE.do(lambda e: e.activation(ov[:, :, :], pV[:, :].rearrange("p (g t) -> p g t", g=2),
                                                        ACT.Copy), tk, last.get("ov"))
                    last["pV"] = to
                    last[("ovt", g // 2)] = to

            LAG = 2
            for i in range(16 + LAG + 1):
                if i < 16:
                    if i % 4 == 0 and 1 <= i // 4 < 3:
                        restack(i // 4 + 1)
                    logits(i)
                    yield
                if 0 <= i - LAG < 16:
                    turn(i - LAG)
                    yield
                if i < 16:
                    exps(i)
                if i - LAG - 1 >= 0 and (i - LAG - 1) % 4 == 3:
                    values((i - LAG - 1) // 4)
                yield
            last["d"] = tlog[15]
            last["vv"] = last[("pt", b * 16 + 15)]
            ta = None
            for q in range(2):
                while not M.free:
                    yield
                bank, free_ = M.get()
                for g in range(4):
                    tk = PE.do(lambda e, g=g, q=q, bank=bank: e.transpose(
                        bank[:, g * 128:g * 128 + 128], OV[g // 2][:, g % 2, q * 128:q * 128 + 128], ident[:, :]),
                        last[("ovt", g // 2)], free_, signal=(g == 3))
                last["ov"] = tk
                v4 = bank[:, :].rearrange("p (h d) -> p h d", d=32)
                tr = DVE.do(lambda e, q=q, v4=v4: e.reciprocal(RC[:, q, :], v4[:, :, 16]), tk, last.get("ao"))
                ta = DVE.do(lambda e, q=q, v4=v4: e.tensor_tensor(
                    AO[:, q, :].rearrange("p (h d) -> p h d", d=16), v4[:, :, 0:16],
                    RC[:, q, :].unsqueeze(2).to_broadcast([128, 16, 16]), ALU.mult), tr)
                rel(bank, ta)
                yield
            ah, al = yield from transposed(AO, ta, CH[:, :, :], CL[:, :, :], last.get("ch"), last.get("ch"))
            last["ao"] = ah
            yield
            while not M.free:
                yield
            bank, free_ = M.get()
            wh, wl = W["o"]
            for t in range(2):
                ts_ = slice(t * 128, t * 128 + 128)
                tk = mm3(bank[:, t * 256:t * 256 + 256],
                         [(CH[:, k, ts_], CL[:, k, ts_], wh[:, k, :], wl[:, k, :]) for k in range(2)],
                         [free_, tok_w["o"], ah, al], t == 1)
            last["ch"] = tk
            b3 = bank[:, :].rearrange("p (t c) -> p t c", t=2)
            ty = DVE.do(lambda e: e.tensor_tensor(X1b[:, :, :], b3, X1b[:, :, :], ALU.add), tk, tx1b)
            rel(bank, ty)
            yield
            x2_tok[b] = normalise(X2, X1b, ty, last.get("x2"), "c")
            last["x1b"] = x2_tok[b]
            yield

        dO = [Stream(f"o{i}") for i in range(2)]
        out_tok = {}

        def stage3(b):
            x2 = X2
            xh, xlo = yield from transposed(x2, x2_tok[b], X2H[:, :, :], X2L[:, :, :], last.get("x2h"),
                                            last.get("x2h"))
            tb = POOL.do(lambda e: e.tensor_tensor(X2b[:, :, :], x2[:, :, :],
                                                   woB[:, :].unsqueeze(1).to_broadcast([128, 2, 256]), ALU.add),
                         x2_tok[b], tok_small, last.get("x2b"))
            last["x2"] = [xh, tb]
            yield
            while not M.free:
                yield
            bank, free_ = M.get()
            tk = mm3(bank[0:40, 0:256], [(GA[0][:, k, :], GA[1][:, k, :], X2H[:, k, :], X2L[:, k, :])
                                         for k in range(2)],
                     [free_, tok_w["g"], free[0], xh, xlo], True)
            tg = ACTE.do(lambda e: e.activation(GS[:, :], bank[0:40, 0:256], ACT.Identity, bias=gate_b[:, :]),
                         tk, last.get("gs"), tok_w["g"])
            rel(bank, tg)
            yield
            while not M.free:
                yield
            bank, free_ = M.get()
            for t in range(2):
                tk = PE.do(lambda e, t=t: e.transpose(bank[:, t * 64:t * 64 + 40], GS[:, t * 128:t * 128 + 128],
                                                      ident[0:40, 0:40]), tg, free_, signal=(t == 1))
            last["gs"] = tk
            gt = bank[:, 0:128].rearrange("p (t c) -> p t c", t=2)
            lg = gt[:, :, 32:40]

            def b8(ap):
                return ap.unsqueeze(2).to_broadcast([128, 2, 8])

            t1 = DVE.do(lambda e: e.tensor_reduce(out=gm[:, 0:2], in_=lg, op=ALU.max, axis=AX.X), tk)
            t1 = DVE.do(lambda e: e.tensor_tensor(g1[:, :, :], lg, b8(gm[:, 0:2]), ALU.is_equal), t1)
            t1 = DVE.do(lambda e: e.tensor_tensor(g1[:, :, :], g1[:, :, :],
                                                  dec8[:, :].unsqueeze(1).to_broadcast([128, 2, 8]), ALU.mult),
                        t1, tok_c)
            t1 = DVE.do(lambda e: e.tensor_reduce(out=gm[:, 2:4], in_=g1[:, :, :], op=ALU.max, axis=AX.X), t1)
            t1 = DVE.do(lambda e: e.tensor_tensor(g2[:, :, :], g1[:, :, :], b8(gm[:, 2:4]), ALU.is_equal), t1)
            for t in range(2):
                t2 = DVE.do(lambda e, t=t: e.tensor_tensor(
                    U2[:, t, :].rearrange("p (e r) -> p e r", r=4),
                    gt[:, t, 0:32].rearrange("p (e r) -> p e r", r=4),
                    g2[:, t, :].unsqueeze(2).to_broadcast([128, 8, 4]), ALU.mult), t1, last.get("u2"))
            rel(bank, t2)
            yield
            while not M.free:
                yield
            bank, free_ = M.get()
            for t in range(2):
                tk = PE.do(lambda e, t=t: e.transpose(bank[0:32, t * 128:t * 128 + 128],
                                                      U2[:, t, :],
                                                      ident[:, :]), t2, free_, signal=(t == 1))
            last["u2"] = tk
            for r in (0, 64):
                th = ACTE.do(lambda e, r=r: e.activation(UL[r:r + 32, :], bank[0:32, 0:256], ACT.Copy), tk,
                             last.get("ul"))
            tl = DVE.do(lambda e: e.tensor_tensor(UL[32:64, :], bank[0:32, 0:256], f(UL[0:32, :]),
                                                  ALU.subtract), th, last.get("ul"))
            tu_ = [th, tl]
            rel(bank, tl)
            yield
            for f2 in range(4):
                while not M.free:
                    yield
                bank, free_ = M.get()
                for i in range(2):
                    c = 2 * f2 + i
                    cs = slice(c * 128, c * 128 + 128)
                    o = bank[:, i * 256:i * 256 + 256]
                    PE.do(lambda e, o=o, cs=cs: e.matmul(o, LB[:, cs], UL[:, :], start=True, stop=False),
                          free_, tu_, *tok_w["lb"], tok_c, signal=False)
                    for k in range(2):
                        for j, (x, y) in enumerate(((WI[0], X2H), (WI[0], X2L), (WI[1], X2H))):
                            e_ = (k == 1 and j == 2)
                            tk = PE.do(lambda e, o=o, cs=cs, x=x, y=y, k=k, e_=e_: e.matmul(
                                o, x[:, k, cs], y[:, k, :], start=False, stop=e_),
                                xh, xlo, tok_w["i"], signal=(e_ and i == 1))
                th = ACTE.do(lambda e, f2=f2, bank=bank: e.activation(IH[:, f2, :], bank[:, :], ACT.Relu), tk,
                             last.get("ih"))
                tl = DVE.do(lambda e, f2=f2, bank=bank: e.scalar_tensor_tensor(
                    out=IL[:, f2, :], in0=bank[:, :], scalar=0.0, in1=f(IH[:, f2, :]), op0=ALU.max,
                    op1=ALU.subtract), th, last.get("ih"))
                rel(bank, tl)
                yield
            last["x2h"] = last["ul"] = tk
            while not M.free:
                yield
            bank, free_ = M.get()
            for t in range(2):
                prs = []
                for c in range(8):
                    o = (c % 2) * 256 + t * 128
                    prs.append((IH[:, c // 2, o:o + 128], IL[:, c // 2, o:o + 128], WP[0][:, c, :], WP[1][:, c, :]))
                for i, (lh, ll, rh, rl) in enumerate(prs):
                    for j, (x, y) in enumerate(((lh, rh), (lh, rl), (ll, rh))):
                        s, e_ = (i == 0 and j == 0), (i == 7 and j == 2)
                        tk = PE.do(lambda e, x=x, y=y, s=s, e_=e_, t=t, bank=bank: e.matmul(
                            bank[:, t * 256:t * 256 + 256], x, y, start=s, stop=e_),
                            free_, th, tl, tok_w["p"], signal=(e_ and t == 1))
                    if i % 2 == 1 and not (i == 7 and t == 1):
                        yield
            last["ih"] = tk
            b3 = bank[:, :].rearrange("p (t c) -> p t c", t=2)
            ty = DVE.do(lambda e: e.tensor_tensor(X2b[:, :, :], b3, X2b[:, :, :], ALU.add), tk, tb)
            rel(bank, ty)
            yield
            tn = normalise(XO[b % 2], X2b, ty, out_tok.get(b - 2), "d")
            last["x2b"] = tn
            out_tok[b] = dO[b % 2].dma(out[b * 256:b * 256 + 256, :].rearrange("(t p) c -> p t c", p=128),
                                       XO[b % 2][:, :, :], tn)
            yield

        def merge(gens):
            live = [[g, n, 0] for g, n in gens]
            while live:
                live.sort(key=lambda x: x[2] / x[1])
                x = live[0]
                try:
                    next(x[0])
                    x[2] += 1
                except StopIteration:
                    live.remove(x)

        merge([(stage1(0), 24), (weights(), 12)])
        for i in range(1, NB + 2):
            gens = []
            if i - 1 < NB:
                gens.append((stage2(i - 1), 68))
            if i < NB:
                gens.append((stage1(i), 24))
            if i - 2 >= 0:
                gens.append((stage3(i - 2), 20))
            merge(gens)
        SP.wait(out_tok[NB - 2], out_tok[NB - 1])

        block = ctx.enter_context(nc.Block())

        @block.sync
        def _(eng):
            SP.run(eng)

        @block.gpsimd
        def _(eng):
            POOL.run(eng)

        @block.scalar
        def _(eng):
            ACTE.run(eng)

        @block.vector
        def _(eng):
            DVE.run(eng)

        @block.tensor
        def _(eng):
            PE.run(eng)


def kernel(**inputs):
    import numpy as np
    import concourse.bacc as bacc
    from concourse import mybir as mb
    from concourse.bass_utils import run_bass_kernel_spmd as run

    i = {k: np.asarray(v) for k, v in inputs.items()}
    fr = i["fside_BxS2_0"]
    arrays = {
        "x": i["x"].reshape(4096, 256),
        "ctxT": i["ctx_1024"].reshape(4096, 256).T,
        "frac": fr,
        "fT": fr.reshape(32, 128).T,
        "kT": i["L0_attn_w_fc"].reshape(1024, 64).T,
        "v": i["L0_attn_w_proj"].T.reshape(1024, 64),
        "ln_g": i["L0_attn_ln_g"],
        "ln_b": i["L0_attn_ln_b"],
        "WqT": i["L0_xattn_Wq"].T,
        "WkT": i["L0_xattn_Wk"].T,
        "WvT": i["L0_xattn_Wv"].T,
        "WoT": i["L0_xattn_Wo"].T,
        "bq": i["L0_xattn_bq"].reshape(2, 128).T,
        "bk": i["L0_xattn_bk"].reshape(2, 128).T,
        "bv": i["L0_xattn_bv"].reshape(2, 128).T,
        "bo": i["L0_xattn_bo"],
        "alpha_pos": i["L0_xattn_alpha_pos"],
        "alpha_neg": i["L0_xattn_alpha_neg"],
        "gamma": i["L0_xattn_gamma"].reshape(1),
        "delta": i["L0_xattn_delta"].reshape(1),
        "gateT": i["L0_ffn_gate_W"].T,
        "gate_b": i["L0_ffn_gate_b"].reshape(8, 1),
        "wiT": i["L0_ffn_wi_W"].T,
        "wi_b": i["L0_ffn_wi_b"],
        "woT": i["L0_ffn_wo_W"].T,
        "wo_b": i["L0_ffn_wo_b"],
        "loraA": i["L0_ffn_lora_A"].reshape(32, 256).T,
        "loraB": i["L0_ffn_lora_B"].transpose(0, 2, 1).reshape(32, 1024),
    }
    arrays = {k: np.ascontiguousarray(v) for k, v in arrays.items()}
    nc = bacc.Bacc("TRN2", target_bir_lowering=False, num_devices=1)
    aps = {k: nc.dram_tensor(f"in_{k}", v.shape, mb.dt.from_np(v.dtype), kind="ExternalInput").ap()
           for k, v in arrays.items()}
    o = nc.dram_tensor("out_0", (4096, 256), mb.dt.float32, kind="ExternalOutput").ap()
    decoder_layer(nc, aps, o)
    r = run(nc, [{f"in_{k}": v for k, v in arrays.items()}], core_ids=[0])
    return r.results[0]["out_0"].reshape(16, 256, 256)
```

```python
import concourse.bass as bass
from concourse import mybir
from contextlib import ExitStack


def decoder_layer(nc, a, out):
    f32 = mybir.dt.float32
    f32r = mybir.dt.float32r
    ALU = mybir.AluOpType
    ACT = mybir.ActivationFunctionType
    AX = mybir.AxisListType

    NB = 16
    EPS = 1e-5
    CLIP = 0.2
    BIG = 3.0e38
    S1, S2A, S2C, S3 = -30, -10, 20, 27

    ctx = ExitStack()
    with ctx:
        def sb(name, shape, dt=f32):
            return ctx.enter_context(nc.sbuf_tensor(name, shape, dt))

        def sem(name):
            return ctx.enter_context(nc.semaphore(name))

        class Later:

            def activation(self, *a, **k):
                return lambda e: e.activation(*a, **k)

            def affine_select(self, *a, **k):
                return lambda e: e.affine_select(*a, **k)

            def bn_aggr(self, *a, **k):
                return lambda e: e.bn_aggr(*a, **k)

            def bn_stats(self, *a, **k):
                return lambda e: e.bn_stats(*a, **k)

            def dma_start(self, *a, **k):
                return lambda e: e.dma_start(*a, **k)

            def matmul(self, *a, **k):
                return lambda e: e.matmul(*a, **k)

            def memset(self, *a, **k):
                return lambda e: e.memset(*a, **k)

            def reciprocal(self, *a, **k):
                return lambda e: e.reciprocal(*a, **k)

            def scalar_tensor_tensor(self, *a, **k):
                return lambda e: e.scalar_tensor_tensor(*a, **k)

            def tensor_copy(self, *a, **k):
                return lambda e: e.tensor_copy(*a, **k)

            def tensor_reduce(self, *a, **k):
                return lambda e: e.tensor_reduce(*a, **k)

            def tensor_scalar(self, *a, **k):
                return lambda e: e.tensor_scalar(*a, **k)

            def tensor_tensor(self, *a, **k):
                return lambda e: e.tensor_tensor(*a, **k)

            def tensor_tensor_reduce(self, *a, **k):
                return lambda e: e.tensor_tensor_reduce(*a, **k)

            def transpose(self, *a, **k):
                return lambda e: e.transpose(*a, **k)

        later = Later()

        class Lane:

            def __init__(self, name):
                self.name, self.sem, self.n, self.queue, self.seen = name, sem("s_" + name), 0, [], {}

            def wait(self, *tokens):
                for t in tokens:
                    if type(t) is list:
                        self.wait(*t)
                    elif t is not None and self.seen.get(t[0].name, 0) < t[1]:
                        self.seen[t[0].name] = t[1]
                        self.queue.append((t[0], t[1], None))

            def do(self, fn, *tokens, signal=True):
                self.wait(*tokens)
                fn = fn(later)
                if not signal:
                    self.queue.append((None, 0, fn))
                    return None
                self.n += 1
                self.queue.append((self.sem, 1, fn))
                return (self.sem, self.n)

            def run(self, eng):
                for s, v, fn in self.queue:
                    if fn is None:
                        eng.wait_ge(s, v)
                    elif s is None:
                        fn(eng)
                    else:
                        fn(eng).then_inc(s, v)

        PE, ACTE, DVE, POOL, SP = (Lane(n) for n in ("pe", "act", "dve", "pool", "sp"))

        class Stream:

            def __init__(self, name):
                self.sem, self.n = sem("d_" + name), 0

            def dma(self, dst, src, *tokens):
                SP.wait(*tokens)
                self.n += 16
                SP.queue.append((self.sem, 16, lambda e: e.dma_start(dst, src)))
                return (self.sem, self.n)

        psum = [ctx.enter_context(nc.psum_tensor(f"bank{i}", [128, 512], f32)) for i in range(8)]
        pL, pT, pV, pA = psum[3:5], psum[5], psum[6], psum[7]

        class Banks:

            def __init__(self):
                self.free = [(psum[i], None) for i in range(3)]

            def get(self):
                return self.free.pop(0)

            def put(self, bank, token):
                self.free.append((bank, token))

        M = Banks()

        def rel(bank, token):
            M.put(bank, token)

        ident = sb("ident", [128, 128])
        KH, KL = sb("KH", [128, 1024], f32r), sb("KL", [128, 1024], f32r)
        VS = sb("VS", [128, 8, 64])
        W = {}
        for n in ("q", "k", "v", "o"):
            W[n] = (sb(f"W{n}h", [128, 2, 256], f32r), sb(f"W{n}l", [128, 2, 256], f32r))
        WI = (sb("WIh", [128, 2, 1024], f32r), sb("WIl", [128, 2, 1024], f32r))
        WP = (sb("WPh", [128, 8, 256], f32r), sb("WPl", [128, 8, 256], f32r))
        GA = (sb("GAh", [128, 2, 40], f32r), sb("GAl", [128, 2, 40], f32r))
        LB = sb("LB", [128, 1024], f32r)
        gB, bB = sb("gB", [128, 256]), sb("bB", [128, 256])
        boB, woB = sb("boB", [128, 256]), sb("woB", [128, 256])
        bqk = sb("bqk", [128, 4])
        bvc = sb("bvc", [128, 2])
        gate_b = sb("gate_b", [40, 1])
        fT = sb("fT", [128, 32])
        alph = sb("alph", [128, 32])
        gd = sb("gd", [128, 2])
        mhalf = sb("mhalf", [128, 2])
        dec8 = sb("dec8", [128, 8])

        NX = 2
        XG = [sb(f"XG{i}", [128, 2, 256]) for i in range(NX)]
        XN = sb("XN", [128, 2, 256])
        SK = sb("SK", [128, 2, 2, 256], f32r)
        NR = 6
        R = [sb(f"R{i}", [128, 512]) for i in range(NR)]
        OT = sb("OT", [128, 2, 256])
        X1 = sb("X1", [128, 2, 256])
        X1b = [sb(f"X1b{i}", [128, 2, 256]) for i in range(2)]
        X1H, X1L = sb("X1H", [128, 2, 256], f32r), sb("X1L", [128, 2, 256], f32r)
        CT = sb("CT", [128, 2, 256])
        CH, CL = sb("CH", [128, 2, 256], f32r), sb("CL", [128, 2, 256], f32r)
        QK = sb("QK", [128, 4, 2, 256], f32r)
        NS = 2
        QS = [sb(f"QS{i}", [128, 2, 4, 256], f32r) for i in range(NS)]
        VV = [sb(f"VV{i}", [128, 2, 16, 32]) for i in range(2)]
        FK = sb("FK", [128, 256])
        dp, dn = sb("DP", [128, 512]), sb("DN", [128, 512])
        NU, NT, NP, NQ = 2, 3, 2, 6
        U = [sb(f"U{i}", [128, 512]) for i in range(NU)]
        T = [sb(f"T{i}", [128, 512]) for i in range(NT)]
        NM = sb("NM", [128, 8, 2])
        P = [sb(f"P{i}", [128, 512]) for i in range(NP)]
        STG = sb("STG", [128, NQ, 512])
        PT = [STG[:, i, :] for i in range(NQ)]
        OV = [sb(f"OV{i}", [128, 2, 256]) for i in range(2)]
        RC = sb("RC", [128, 2, 16])
        AO = sb("AO", [128, 2, 256])
        X2 = sb("X2", [128, 2, 256])
        X2b = sb("X2b", [128, 2, 256])
        X2H, X2L = sb("X2H", [128, 2, 256], f32r), sb("X2L", [128, 2, 256], f32r)
        GS = sb("GS", [40, 256])
        g1, g2 = sb("g1", [128, 2, 8]), sb("g2", [128, 2, 8])
        gm = sb("gm", [128, 4])
        U2 = sb("U2", [128, 2, 32])
        UL = sb("UL", [128, 256], f32r)
        IH, IL = sb("IH", [128, 4, 512], f32r), sb("IL", [128, 4, 512], f32r)
        XO = sb("XO", [128, 2, 256])
        SM = {k: sb("SM" + k, [128, 24]) for k in "abcd"}

        def f(ap):
            return ap.bitcast(f32)

        def split(hi, lo, src, src_tok, hi_free, lo_free):
            th = ACTE.do(lambda e: e.activation(hi, src, ACT.Copy), src_tok, hi_free)
            tl = DVE.do(lambda e: e.tensor_tensor(lo, src, f(hi), ALU.subtract), th, src_tok, lo_free)
            return th, tl

        def normalise(dst, src, src_tok, dst_free, k):
            s = SM[k]
            st = s[:, 0:12].rearrange("p (t c) -> p t c", t=2)
            mv = s[:, 12:16].rearrange("p (t c) -> p t c", t=2)
            for t in range(2):
                tk = DVE.do(lambda e, t=t: e.bn_stats(st[:, t, :], src[:, t, :]), src_tok)
            for t in range(2):
                tk = DVE.do(lambda e, t=t: e.bn_aggr(mv[:, t, :], st[:, t, :]), tk)
            tk = DVE.do(lambda e: e.tensor_scalar(s[:, 16:18], mv[:, :, 1], EPS, None, ALU.add), tk)
            yield 0.50
            tk = POOL.do(lambda e: e.tensor_tensor(s[:, 18:20], s[:, 16:18], mhalf[:, :], ALU.pow), tk)
            yield 0.90
            for t in range(2):
                last = DVE.do(lambda e, t=t: e.tensor_scalar(dst[:, t, :], src[:, t, :], mv[:, t, 0:1],
                                                             s[:, 18 + t:19 + t], ALU.subtract, ALU.mult),
                              tk, dst_free)
            return last

        def transposed(src, src_tok, hi, lo, hi_free, lo_free):
            while not M.free:
                yield
            bank, free = M.get()
            for m in range(2):
                for t in range(2):
                    tk = PE.do(lambda e, m=m, t=t: e.transpose(
                        bank[:, m * 256 + t * 128:m * 256 + t * 128 + 128],
                        src[:, t, m * 128:m * 128 + 128], ident[:, :]), src_tok, free, signal=(m + t == 2))
            b3 = bank[:, :].rearrange("p (m t) -> p m t", m=2)
            yield 0.30
            th = ACTE.do(lambda e: e.activation(hi, b3, ACT.Copy), tk, hi_free)
            yield 0.30
            tl = DVE.do(lambda e: e.tensor_tensor(lo, b3, f(hi), ALU.subtract), th, lo_free)
            rel(bank, tl)
            yield 0.30
            return th, tl

        def mm3(bank_ap, pairs, tokens, signal):
            n = len(pairs)
            tk = None
            for i, (lh, ll, rh, rl) in enumerate(pairs):
                for j, (x, y) in enumerate(((lh, rh), (lh, rl), (ll, rh))):
                    s, e_ = (i == 0 and j == 0), (i == n - 1 and j == 2)
                    tk = PE.do(lambda e, x=x, y=y, s=s, e_=e_: e.matmul(bank_ap, x, y, start=s, stop=e_),
                               *tokens, signal=signal and e_)
            return tk

        last = {}
        done = set()

        dS = Stream("small")
        tok_small = None
        for dst, src in ((gB, a["ln_g"]), (bB, a["ln_b"]), (boB, a["bo"]), (woB, a["wo_b"])):
            tok_small = dS.dma(dst[:, :], src.partition_broadcast(128))
        tok_small = dS.dma(alph[:, 0:16], a["alpha_pos"].partition_broadcast(128))
        tok_small = dS.dma(alph[:, 16:32], a["alpha_neg"].partition_broadcast(128))
        tok_small = dS.dma(gd[:, 0:1], a["gamma"].partition_broadcast(128))
        tok_small = dS.dma(gd[:, 1:2], a["delta"].partition_broadcast(128))
        tok_small = dS.dma(bqk[:, 0:2], a["bq"])
        tok_small = dS.dma(bqk[:, 2:4], a["bk"])
        tok_small = dS.dma(bvc[:, :], a["bv"])
        tok_small = dS.dma(fT[:, :], a["fT"])
        tok_small = dS.dma(VS[:, :, :], a["v"].rearrange("(c p) d -> p c d", p=128))

        tk = POOL.do(lambda e: e.memset(ident[:, :], 0.0))
        tok_id = POOL.do(lambda e: e.affine_select(out=ident[:, :], in_=ident[:, :], compare_op=ALU.not_equal,
                                                   fill=1.0, base=0, pattern=[[-1, 128]],
                                                   channel_multiplier=1), tk)
        tok_mh = POOL.do(lambda e: e.memset(mhalf[:, :], -0.5))
        POOL.do(lambda e: e.memset(gate_b[:, :], 0.0))
        for i in range(8):
            tok_c = POOL.do(lambda e, i=i: e.memset(dec8[:, i:i + 1], float(8 - i)))
        tok_c = POOL.do(lambda e: e.memset(f(UL[96:128, :]), 1.0), tok_c)
        tok_lbz = POOL.do(lambda e: e.memset(f(LB[96:128, :]), 0.0), tok_c)
        for i in range(2):
            tok_c = POOL.do(lambda e, i=i: e.memset(VV[i][:, :, :, 16:32], 0.0), tok_lbz)
            tok_c = POOL.do(lambda e, i=i: e.memset(VV[i][:, :, :, 16:17], 1.0), tok_c)
        for t in QS:
            tok_zero = POOL.do(lambda e, t=t: e.memset(f(t[:, :, :, :]), 0.0))

        dX, dC, dF = [Stream(f"x{i}") for i in range(NX)], Stream("c"), Stream("f")

        def load_x(b, free):
            return dX[b % NX].dma(XG[b % NX][:, :, :],
                                 a["x"][b * 256:b * 256 + 256, :].rearrange("(t p) c -> p t c", p=128), free)

        def load_c(b, free):
            return dC.dma(CT[:, :, :],
                                 a["ctxT"][:, b * 256:b * 256 + 256].rearrange("(k p) t -> p k t", p=128), free)

        def load_f(b, free):
            return dF.dma(FK[:, :], a["frac"][b, :].partition_broadcast(128), free)

        xl, cl, fl = {0: load_x(0, None)}, {}, {}

        def stage(n_cols, slot):
            return STG[:, slot:slot + (n_cols + 511) // 512, :].rearrange("p a b -> p (a b)")[:, 0:n_cols]

        dW = [Stream(f"w{i}") for i in range(3)]
        reg = [(0, 2), (2, 2), (4, 2)]
        jobs = []
        free = [None, None, None]

        def weight(i, src_ap, parts, shape, hi, lo, scale=None, scale_tok=None):
            st = stage(shape[0] * shape[1], reg[i][0])[0:parts, :]
            v = st.rearrange("p (a b) -> p a b", a=shape[0])
            tk = dW[i].dma(v, src_ap, free[i])
            if scale is not None:
                tk = DVE.do(lambda e: e.tensor_scalar(v, v, scale[0:parts, :], 0.25, ALU.mult, ALU.mult),
                            tk, scale_tok)
            th, tl = split(hi, lo, v, tk, None, None)
            free[i] = tl
            return tl

        st = stage(1024, 0)
        dW[0].dma(st[0:64, :], a["kT"])
        tk = dW[0].dma(st[64:128, :], a["kT"])
        tok_kh, tok_k = split(KH[:, :], KL[:, :], st, tk, None, None)
        free[0] = tok_k

        def col(src, k):
            return src.rearrange("(k p) e -> p k e", p=128)

        tok_w = {}

        def weights():
            nonlocal tok_small, tok_c
            t1 = DVE.do(lambda e: e.tensor_scalar(bqk[:, 0:2], bqk[:, 0:2], gd[:, 0:1], 0.25, ALU.mult, ALU.mult),
                        (dS.sem, dS.n))
            t2 = DVE.do(lambda e: e.tensor_scalar(alph[:, :], alph[:, :], gd[:, 1:2], None, ALU.mult))
            tok_w["small"] = t2
            tok_w["v"] = weight(1, col(a["WvT"], 2), 128, (2, 256), W["v"][0][:, :, :], W["v"][1][:, :, :])
            yield
            tok_w["k"] = weight(2, col(a["WkT"], 2), 128, (2, 256), W["k"][0][:, :, :], W["k"][1][:, :, :])
            yield
            tok_w["q"] = weight(0, col(a["WqT"], 2), 128, (2, 256), W["q"][0][:, :, :], W["q"][1][:, :, :],
                                gd[:, 0:1], (dS.sem, dS.n))
            yield
            st = stage(512, reg[1][0])
            v = st.rearrange("p (a b) -> p a b", a=2)
            tk = dW[1].dma(v, col(a["WoT"], 2), free[1])
            th, tl = split(W["o"][0][:, :, :], W["o"][1][:, :, :], v, tk, None, None)
            while not M.free:
                yield
            bank, bf = M.get()
            for k in range(2):
                tp = PE.do(lambda e, k=k: e.matmul(bank[:, 0:256], bvc[:, k:k + 1].to_broadcast([128, 128]),
                                                   v[:, k, :], start=(k == 0), stop=(k == 1)),
                           bf, tk, (dS.sem, dS.n), signal=(k == 1))
            t3 = DVE.do(lambda e: e.tensor_tensor(boB[:, :], boB[:, :], bank[:, 0:256], ALU.add), tp)
            rel(bank, t3)
            free[1] = t3
            tok_w["o"] = t3
            yield
            for h in range(2):
                tok_w["i"] = weight(2 * h, a["wiT"][h * 128:h * 128 + 128, :].rearrange("p (a e) -> p a e", a=1),
                                    128, (1, 1024), WI[0][:, h:h + 1, :], WI[1][:, h:h + 1, :])
                yield
            for h in range(2):
                tok_w["p"] = weight(1 + h, a["woT"][h * 512:h * 512 + 512, :].rearrange("(k p) e -> p k e", p=128),
                                    128, (4, 256), WP[0][:, 4 * h:4 * h + 4, :], WP[1][:, 4 * h:4 * h + 4, :])
                yield
            st = stage(80, reg[0][0])
            v = st.rearrange("p (a b) -> p a b", a=2)
            dW[0].dma(v[:, :, 0:32], col(a["loraA"], 2), free[0])
            tk = dW[0].dma(v[:, :, 32:40], col(a["gateT"], 2))
            th, tl = split(GA[0][:, :, :], GA[1][:, :, :], v, tk, None, None)
            free[0] = tl
            tok_w["g"] = dS.dma(gate_b[32:40, :], a["gate_b"], tok_c)
            yield
            st = stage(1024, reg[1][0])
            for r in range(3):
                tk = dW[1].dma(st[32 * r:32 * r + 32, :], a["loraB"], free[1])
            th = ACTE.do(lambda e: e.activation(LB[0:96, :], st[0:96, :], ACT.Copy), tk)
            tl = DVE.do(lambda e: e.tensor_tensor(LB[64:96, :], st[64:96, :], f(LB[64:96, :]), ALU.subtract), th)
            bh, bl = IH[0:1, 0:2, :], IL[0:1, 0:2, :]
            st2 = stage(1024, reg[2][0])[0:1, :].rearrange("p (a b) -> p a b", a=2)
            tk = dW[2].dma(st2, a["wi_b"].rearrange("(o a b) -> o a b", o=1, a=2), free[2])
            th2, tl2 = split(bh, bl, st2, tk, None, None)
            t4 = dW[1].dma(f(LB[96:97, :]).rearrange("p (a b) -> p a b", a=2), f(bh), th2, tl2, tok_lbz)
            t4 = dW[1].dma(f(LB[97:98, :]).rearrange("p (a b) -> p a b", a=2), f(bl))
            tok_w["lb"] = (th, tl, t4)
            free[1] = free[2] = tl
            tok_w["stage"] = [tl, tl2, tok_w["g"]]
            yield

        x1_tok, x1t_tok = {}, {}

        def stage1(b):
            xg = XG[b % NX]
            if b == 0:
                cl[0], fl[0] = load_c(0, None), load_f(0, None)
            tx = yield from normalise(XN, xg, xl[b], last.get("xn"), "a")
            gb = gB[:, :].unsqueeze(1).to_broadcast([128, 2, 256])
            bb = bB[:, :].unsqueeze(1).to_broadcast([128, 2, 256])
            tx = DVE.do(lambda e: e.tensor_tensor(XN[:, :, :], XN[:, :, :], gb, ALU.mult), tx, tok_small)
            tx = DVE.do(lambda e: e.tensor_tensor(XN[:, :, :], XN[:, :, :], bb, ALU.add), tx)
            yield 0.80
            while b > 0 and ("1", b - 1) not in done:
                yield 0.10
            if b + 1 < NB:
                xl[b + 1] = load_x(b + 1, last.get(("y1", b + 1 - NX)))
            while not M.free:
                yield
            bank, free_ = M.get()
            for hp in range(2):
                for t in range(2):
                    tk = PE.do(lambda e, hp=hp, t=t, bank=bank: e.transpose(
                        bank[:, hp * 256 + t * 128:hp * 256 + t * 128 + 128],
                        XN[:, t, hp * 128:hp * 128 + 128], ident[:, :]),
                        tx, free_, tok_id, signal=(hp + t == 2))
            last["xn"] = tk
            b3 = bank[:, :].rearrange("p (h t) -> p h t", h=2)
            yield 0.20
            for h in range(2):
                own, other = slice(64 * h, 64 * h + 64), slice(64 - 64 * h, 128 - 64 * h)
                th = ACTE.do(lambda e, h=h, own=own, b3=b3: e.activation(SK[own, :, h, :], b3[own, :, :], ACT.Copy),
                             tk, last.get("sk"))
            yield 0.30
            for h in range(2):
                own, other = slice(64 * h, 64 * h + 64), slice(64 - 64 * h, 128 - 64 * h)
                tl = DVE.do(lambda e, h=h, own=own, other=other, b3=b3: e.tensor_tensor(
                    SK[other, :, h, :], b3[own, :, :], f(SK[own, :, h, :]), ALU.subtract), th)
            rel(bank, tl)
            sk_tok = [th, tl]
            yield 0.50
            units = [(hp, c2, h) for hp in range(2) for c2 in range(4) for h in range(2)]
            sq = {}

            def av(j):
                hp, c2, _ = units[2 * j]
                for i in range(2):
                    for h in range(2):
                        r, ts = sq[2 * j + h]
                        c = 2 * c2 + i
                        tk = PE.do(lambda e, r=r, i=i, h=h, c=c, hp=hp: e.matmul(
                            pA[64 * h:64 * h + 64, hp * 256:hp * 256 + 256], VS[:, c, :],
                            r[:, i * 256:i * 256 + 256], start=(c == 0), stop=(c == 7),
                            skip_group_check=True),
                            ts, last.get("pA"), signal=(i == 1 and h == 1))
                for h in range(2):
                    last[("r", (last["rn"][2 * j + h]))] = tk
                return tk

            last["rn"] = {}
            for u, (hp, c2, h) in enumerate(units):
                while not M.free:
                    yield
                bank, free_ = M.get()
                for i in range(2):
                    c = 2 * c2 + i
                    for n, kk in enumerate((KH, KL)):
                        tk = PE.do(lambda e, bank=bank, i=i, c=c, kk=kk, n=n, hp=hp, h=h: e.matmul(
                            bank[:, i * 256:i * 256 + 256], kk[:, c * 128:c * 128 + 128], SK[:, hp, h, :],
                            start=(n == 0), stop=(n == 1)),
                            free_, sk_tok, tok_kh, tok_k, signal=(i == 1 and n == 1))
                last["sk"] = tk
                slot = (b * 16 + u) % NR
                r = R[slot]
                last["rn"][u] = slot
                tr = ACTE.do(lambda e, r=r, bank=bank: e.activation(r[:, :], bank[:, :], ACT.Relu), tk,
                             last.get(("r", slot)))
                rel(bank, tr)
                lane = DVE if u % 8 == 7 else POOL
                ts = lane.do(lambda e, r=r: e.tensor_tensor(r[:, :], r[:, :], r[:, :], ALU.mult), tr)
                sq[u] = (r, ts)
                if u % 2 == 1 and u >= 5:
                    av(u // 2 - 2)
                yield 0.66
            av(6)
            yield 0.01
            tk = av(7)
            yield 0.30
            to = ACTE.do(lambda e: e.activation(OT[:, :, :], pA[:, :].rearrange("p (h t) -> p h t", h=2),
                                                ACT.Copy), tk, last.get("ot"))
            last["pA"] = to
            yield 0.30
            while not M.free:
                yield
            bank, free_ = M.get()
            for t in range(2):
                for hp in range(2):
                    tk = PE.do(lambda e, t=t, hp=hp: e.transpose(
                        bank[:, t * 256 + hp * 128:t * 256 + hp * 128 + 128],
                        OT[:, hp, t * 128:t * 128 + 128], ident[:, :]), to, free_, signal=(t + hp == 2))
            last["ot"] = tk
            yield 0.30
            b3 = bank[:, :].rearrange("p (t c) -> p t c", t=2)
            ty = DVE.do(lambda e: e.scalar_tensor_tensor(out=xg[:, :, :], in0=xg[:, :, :], scalar=2.0, in1=b3,
                                                         op0=ALU.mult, op1=ALU.add), tk)
            rel(bank, ty)
            yield
            x1_tok[b] = yield from normalise(X1, xg, ty, last.get("x1"), "b")
            last[("y1", b)] = x1_tok[b]
            done.add(("1", b))
            yield

        dQ = [Stream(f"q{i}") for i in range(NS)]
        x2_tok = {}

        tok_d, tok_v, st_tok, qk_free = {}, {}, {}, {-1: None}
        tlg, tu, tlog, texp, tturn, tev = {}, {}, {}, {}, {}, {}

        def differences(b):
            for q in range(2):
                td = DVE.do(lambda e, q=q: e.tensor_scalar(dn[:, q * 256:q * 256 + 256], FK[:, :],
                                                           fT[:, 2 * b + q:2 * b + q + 1], CLIP,
                                                           ALU.subtract, ALU.min), fl[b], tlog.get(16 * b - 1))
            if b + 1 < NB:
                fl[b + 1] = load_f(b + 1, td)
            tdp = DVE.do(lambda e: e.tensor_scalar(dp[:, :], dn[:, :], 0.0, None, ALU.max), td)
            tdn = DVE.do(lambda e: e.tensor_scalar(dn[:, :], dn[:, :], -CLIP, 0.0, ALU.max, ALU.min), tdp)
            tok_d[b] = (tdp, tdn)

        def stage2a(b):
            while b not in x1_tok or (b >= 2 and ("2c", b - 2) not in done):
                yield
            th = ACTE.do(lambda e: e.activation(CH[:, :, :], CT[:, :, :], ACT.Copy), cl[b], last.get("ch"))
            yield 0.50
            tl = DVE.do(lambda e: e.tensor_tensor(CL[:, :, :], CT[:, :, :], f(CH[:, :, :]), ALU.subtract), th)
            if b + 1 < NB:
                cl[b + 1] = load_c(b + 1, tl)
            yield 0.10
            xh, xlo = yield from transposed(X1, x1_tok[b], X1H[:, :, :], X1L[:, :, :],
                                            last.get("x1h"), last.get("x1h"))
            tx1b = POOL.do(lambda e: e.tensor_tensor(X1b[b % 2][:, :, :], X1[:, :, :],
                                                     boB[:, :].unsqueeze(1).to_broadcast([128, 2, 256]), ALU.add),
                           x1_tok[b], tok_w["o"], last.get(("x1b", b - 2)))
            last["x1"] = [xh, tx1b]
            last[("tx1b", b)] = tx1b
            yield

            def project(n, src, toks, bias, hi, lo, key):
                while not M.free:
                    yield
                bank, free_ = M.get()
                wh, wl = W[n]
                for m in range(2):
                    cs = slice(m * 128, m * 128 + 128)
                    tk = mm3(bank[:, m * 256:m * 256 + 256],
                             [(wh[:, k, cs], wl[:, k, cs], src[0][:, k, :], src[1][:, k, :]) for k in range(2)],
                             [free_, tok_w[n], *toks], m == 1)
                yield 0.45
                for m in range(2):
                    bm = bank[:, m * 256:m * 256 + 256]
                    th = ACTE.do(lambda e, m=m, bm=bm: e.activation(hi[:, m, :], bm, ACT.Identity,
                                                                    bias=bqk[:, bias + m:bias + m + 1]),
                                 tk, last.get(key), tok_w["small"])
                yield 0.40
                for m in range(2):
                    bm = bank[:, m * 256:m * 256 + 256]
                    tl = DVE.do(lambda e, m=m, bm=bm: e.scalar_tensor_tensor(
                        out=lo[:, m, :], in0=bm, scalar=bqk[:, bias + m:bias + m + 1], in1=f(hi[:, m, :]),
                        op0=ALU.add, op1=ALU.subtract), th, last.get(key))
                rel(bank, tl)
                return th, tl, tk

            while b - 1 not in qk_free:
                yield
            kt = yield from project("k", (CH, CL), (th, tl), 2, QK[:, 2], QK[:, 3], "qk")
            yield
            qt = yield from project("q", (X1H, X1L), (xh, xlo), 0, QK[:, 1], QK[:, 0], "qk")
            last["x1h"] = qt[2]
            made[b] = [kt[0], kt[1], qt[0], qt[1]]
            yield
            while not M.free:
                yield
            bank, free_ = M.get()
            wh, wl = W["v"]
            for t in range(2):
                ts_ = slice(t * 128, t * 128 + 128)
                tk = mm3(bank[:, t * 256:t * 256 + 256],
                         [(CH[:, k, ts_], CL[:, k, ts_], wh[:, k, :], wl[:, k, :]) for k in range(2)],
                         [free_, tok_w["v"], th, tl], t == 1)
            last["ch"] = tk
            for t in range(2):
                tv = DVE.do(lambda e, t=t: e.tensor_copy(
                    VV[b % 2][:, t, :, 0:16], bank[:, t * 256:t * 256 + 256].rearrange("p (h d) -> p h d", h=16)),
                    tk, last.get(("pt", 16 * (b - 1) - 1)), tok_c)
            rel(bank, tv)
            tok_v[b] = tv
            done.add(("2a", b))
            yield

        made = {}

        def restack(G):
            b, g = G // 4, G % 4
            s = G % NS
            for r, (q, k) in enumerate(((1, 2), (0, 2), (1, 3))):
                for j in range(2):
                    p = 32 * g + 16 * j
                    tk = dQ[s].dma(f(QS[s][16 * r:16 * r + 16, :, 2 * j:2 * j + 2, :]).rearrange("p a m t -> p a (m t)"),
                                   f(QK[p:p + 16, q:k + 1:k - q, :, :]).rearrange("p a m t -> p a (m t)"),
                                   *made[b], last.get(("qs", s)), tok_zero)
            st_tok[G] = tk
            if g == 3:
                last["qk"] = tk
                qk_free[b] = tk

        def head(n):
            return (n % 16) // 2 + 8 * (n % 2)

        def logits(n):
            b, h = n // 16, head(n)
            tdp = tok_d[b][0]
            s, L = (n // 4) % NS, pL[n % 2]
            for q in range(2):
                tk = PE.do(lambda e, q=q: e.matmul(L[:, q * 256:q * 256 + 256],
                                                   QS[s][:, 0, n % 4, q * 128:q * 128 + 128],
                                                   QS[s][:, 1, n % 4, :],
                                                   start=True, stop=True),
                           st_tok[n // 4], last.get(("L", n - 2)), signal=(q == 1))
            last[("qs", s)] = tk
            tlg[n] = tk
            u = U[n % NU]
            tu[n] = POOL.do(lambda e: e.tensor_scalar(u[:, :], dp[:, :], alph[:, h:h + 1], 0.0, ALU.mult, ALU.add),
                            tdp, last.get(("u", n - NU)), tok_w["small"])

        def biased(n):
            h, L, u, t = head(n), pL[n % 2], U[n % NU], T[n % NT]
            t1 = DVE.do(lambda e: e.scalar_tensor_tensor(out=t[:, :], in0=dn[:, :],
                                                         scalar=alph[:, 16 + h:17 + h], in1=L[:, :],
                                                         op0=ALU.mult, op1=ALU.add),
                        tlg[n], tok_d[n // 16][1], last.get(("t", n - NT)))
            last[("L", n)] = t1
            for q in range(2):
                cs = slice(q * 256, q * 256 + 256)
                t2 = DVE.do(lambda e, q=q, cs=cs: e.tensor_tensor_reduce(
                    out=t[:, cs], in0=t[:, cs], in1=u[:, cs], scale=-1.0, scalar=BIG, op0=ALU.add,
                    op1=ALU.min, accum_out=NM[:, n % 8, q:q + 1]), t1, tu[n], last.get(("t", n - 8)))
            last[("u", n)] = t2
            tlog[n] = t2

        def exps(n):
            t, p = T[n % NT], P[n % NP]
            for q in range(2):
                cs = slice(q * 256, q * 256 + 256)
                tk = ACTE.do(lambda e, q=q, cs=cs: e.activation(p[:, cs], t[:, cs], ACT.Exp,
                                                                bias=NM[:, n % 8, q:q + 1], scale=-1.0),
                             tlog[n], last.get(("p", n - NP)))
            last[("t", n)] = tk
            texp[n] = tk

        def turn(n):
            p = P[n % NP]
            for k in range(2):
                for q in range(2):
                    tk = PE.do(lambda e, k=k, q=q: e.transpose(
                        pT[:, k * 256 + q * 128:k * 256 + q * 128 + 128],
                        p[:, q * 256 + k * 128:q * 256 + k * 128 + 128], ident[:, :]),
                        texp[n], last.get("pT"), signal=(k + q == 2))
            last[("p", n)] = tturn[n] = tk

        def turned(n):
            pt, tk = PT[n % NQ], tturn[n]
            extra = tok_w["stage"] if n < NQ else ()
            tev[n] = ACTE.do(lambda e: e.activation(pt, pT[:, :], ACT.Copy), tk, last.get(("pt", n - NQ)),
                             *extra)
            last["pT"] = tev[n]

        def values(G):
            b, g = G // 4, G % 4
            c0 = (g % 2) * 256
            for k in range(2):
                for j in range(4):
                    n = 4 * G + j
                    tk = PE.do(lambda e, k=k, j=j, n=n: e.matmul(
                        pV[32 * j:32 * j + 32, c0:c0 + 256], VV[b % 2][:, k, head(n), :],
                        PT[n % NQ][:, k * 256:k * 256 + 256],
                        start=(k == 0), stop=(k == 1), skip_group_check=True),
                        tev[n], tok_v[b], last.get("pV"), signal=(k == 1 and j == 3))
            for j in range(4):
                last[("pt", 4 * G + j)] = tk
            if g % 2:
                ov = OV[g // 2]
                to = ACTE.do(lambda e: e.activation(ov[:, :, :], pV[:, :].rearrange("p (g t) -> p g t", g=2),
                                                    ACT.Copy), tk, last.get("ov"))
                last["pV"] = to
                last[("ovt", b, g // 2)] = to

        def attention():
            N = NB * 16
            for n in range(N + 5):
                if n < N:
                    if n % 4 == 0 and n // 4 + 1 < NB * 4:
                        while n == 0 and 0 not in made:
                            yield 0.10
                        if n == 0:
                            restack(0)
                        while (n // 4 + 1) // 4 not in made:
                            yield 0.50
                        restack(n // 4 + 1)
                    if n % 16 == 0:
                        while ("2a", n // 16) not in done:
                            yield 0.41
                        if n:
                            biased(n - 1)
                        differences(n // 16)
                    logits(n)
                yield 0.20
                if 1 <= n <= N and (n % 16 or n == N):
                    biased(n - 1)
                yield 0.20
                if 3 <= n < N + 3:
                    turn(n - 3)
                yield 0.20
                if 2 <= n < N + 2:
                    exps(n - 2)
                yield 0.20
                if 3 <= n < N + 3:
                    turned(n - 3)
                if n >= 4 and (n - 4) % 4 == 3:
                    values((n - 4) // 4)
                yield 0.20

        def stage2c(b):
            while ("ovt", b, 1) not in last or (b + 1 < NB and ("2a", b + 1) not in done):
                yield
            ta = None
            for q in range(2):
                while not M.free:
                    yield
                bank, free_ = M.get()
                for g in range(4):
                    tk = PE.do(lambda e, g=g, q=q, bank=bank: e.transpose(
                        bank[:, g * 128:g * 128 + 128], OV[g // 2][:, g % 2, q * 128:q * 128 + 128], ident[:, :]),
                        last[("ovt", b, g // 2)], free_, signal=(g == 3))
                last["ov"] = tk
                yield 0.30
                v4 = bank[:, :].rearrange("p (h d) -> p h d", d=32)
                tr = DVE.do(lambda e, q=q, v4=v4: e.reciprocal(RC[:, q, :], v4[:, :, 16]), tk, last.get("ao"))
                ta = DVE.do(lambda e, q=q, v4=v4: e.tensor_tensor(
                    AO[:, q, :].rearrange("p (m h d) -> p h m d", m=2, d=16),
                    v4[:, :, 0:16].rearrange("p (h m) d -> p h m d", m=2),
                    RC[:, q, :].rearrange("p (h m) -> p h m", m=2).unsqueeze(3).to_broadcast([128, 8, 2, 16]),
                    ALU.mult), tr)
                rel(bank, ta)
                yield 0.30
            ah, al = yield from transposed(AO, ta, CH[:, :, :], CL[:, :, :], last.get("ch"), last.get("ch"))
            last["ao"] = ah
            while not M.free:
                yield
            bank, free_ = M.get()
            wh, wl = W["o"]
            for t in range(2):
                ts_ = slice(t * 128, t * 128 + 128)
                tk = mm3(bank[:, t * 256:t * 256 + 256],
                         [(CH[:, k, ts_], CL[:, k, ts_], wh[:, k, :], wl[:, k, :]) for k in range(2)],
                         [free_, tok_w["o"], ah, al], t == 1)
            last["ch"] = tk
            yield 0.50
            b3 = bank[:, :].rearrange("p (t c) -> p t c", t=2)
            ty = DVE.do(lambda e: e.tensor_tensor(X1b[b % 2][:, :, :], b3, X1b[b % 2][:, :, :], ALU.add),
                        tk, last[("tx1b", b)])
            rel(bank, ty)
            yield
            x2_tok[b] = yield from normalise(X2, X1b[b % 2], ty, last.get("x2"), "c")
            last[("x1b", b)] = x2_tok[b]
            done.add(("2c", b))
            yield

        dO = Stream("o")
        out_tok = {}

        def stage3(b):
            while b not in x2_tok:
                yield
            x2 = X2
            xh, xlo = yield from transposed(x2, x2_tok[b], X2H[:, :, :], X2L[:, :, :], last.get("x2h"),
                                            last.get("x2h"))
            tb = POOL.do(lambda e: e.tensor_tensor(X2b[:, :, :], x2[:, :, :],
                                                   woB[:, :].unsqueeze(1).to_broadcast([128, 2, 256]), ALU.add),
                         x2_tok[b], tok_small, last.get("x2b"))
            last["x2"] = [xh, tb]
            yield
            while not M.free:
                yield
            bank, free_ = M.get()
            tk = mm3(bank[0:40, 0:256], [(GA[0][:, k, :], GA[1][:, k, :], X2H[:, k, :], X2L[:, k, :])
                                         for k in range(2)],
                     [free_, tok_w["g"], free[0], xh, xlo], True)
            yield 0.40
            tg = ACTE.do(lambda e: e.activation(GS[:, :], bank[0:40, 0:256], ACT.Identity, bias=gate_b[:, :]),
                         tk, last.get("gs"), tok_w["g"])
            rel(bank, tg)
            yield 0.25
            while not M.free:
                yield
            bank, free_ = M.get()
            for t in range(2):
                tk = PE.do(lambda e, t=t: e.transpose(bank[:, t * 64:t * 64 + 40], GS[:, t * 128:t * 128 + 128],
                                                      ident[0:40, 0:40]), tg, free_, signal=(t == 1))
            last["gs"] = tk
            yield 0.30
            gt = bank[:, 0:128].rearrange("p (t c) -> p t c", t=2)
            lg = gt[:, :, 32:40]

            def b8(ap):
                return ap.unsqueeze(2).to_broadcast([128, 2, 8])

            t1 = DVE.do(lambda e: e.tensor_reduce(out=gm[:, 0:2], in_=lg, op=ALU.max, axis=AX.X), tk)
            t1 = DVE.do(lambda e: e.tensor_tensor(g1[:, :, :], lg, b8(gm[:, 0:2]), ALU.is_equal), t1)
            t1 = DVE.do(lambda e: e.tensor_tensor(g1[:, :, :], g1[:, :, :],
                                                  dec8[:, :].unsqueeze(1).to_broadcast([128, 2, 8]), ALU.mult),
                        t1, tok_c)
            t1 = DVE.do(lambda e: e.tensor_reduce(out=gm[:, 2:4], in_=g1[:, :, :], op=ALU.max, axis=AX.X), t1)
            t1 = DVE.do(lambda e: e.tensor_tensor(g2[:, :, :], g1[:, :, :], b8(gm[:, 2:4]), ALU.is_equal), t1)
            for t in range(2):
                t2 = DVE.do(lambda e, t=t: e.tensor_tensor(
                    U2[:, t, :].rearrange("p (e r) -> p e r", r=4),
                    gt[:, t, 0:32].rearrange("p (e r) -> p e r", r=4),
                    g2[:, t, :].unsqueeze(2).to_broadcast([128, 8, 4]), ALU.mult), t1, last.get("u2"))
            rel(bank, t2)
            yield 0.55
            while not M.free:
                yield
            bank, free_ = M.get()
            for t in range(2):
                tk = PE.do(lambda e, t=t: e.transpose(bank[0:32, t * 128:t * 128 + 128],
                                                      U2[:, t, :],
                                                      ident[:, :]), t2, free_, signal=(t == 1))
            last["u2"] = tk
            yield 0.20
            for r in (0, 64):
                th = ACTE.do(lambda e, r=r: e.activation(UL[r:r + 32, :], bank[0:32, 0:256], ACT.Copy), tk,
                             last.get("ul"))
            yield 0.70
            tl = DVE.do(lambda e: e.tensor_tensor(UL[32:64, :], bank[0:32, 0:256], f(UL[0:32, :]),
                                                  ALU.subtract), th, last.get("ul"))
            tu_ = [th, tl]
            rel(bank, tl)
            yield 0.30
            for f2 in range(4):
                while not M.free:
                    yield
                bank, free_ = M.get()
                for i in range(2):
                    c = 2 * f2 + i
                    cs = slice(c * 128, c * 128 + 128)
                    o = bank[:, i * 256:i * 256 + 256]
                    PE.do(lambda e, o=o, cs=cs: e.matmul(o, LB[:, cs], UL[:, :], start=True, stop=False),
                          free_, tu_, *tok_w["lb"], tok_c, signal=False)
                    for k in range(2):
                        for j, (x, y) in enumerate(((WI[0], X2H), (WI[0], X2L), (WI[1], X2H))):
                            e_ = (k == 1 and j == 2)
                            tk = PE.do(lambda e, o=o, cs=cs, x=x, y=y, k=k, e_=e_: e.matmul(
                                o, x[:, k, cs], y[:, k, :], start=False, stop=e_),
                                xh, xlo, tok_w["i"], signal=(e_ and i == 1))
                th = ACTE.do(lambda e, f2=f2, bank=bank: e.activation(IH[:, f2, :], bank[:, :], ACT.Relu), tk,
                             last.get("ih"))
                yield 0.40
                tl = DVE.do(lambda e, f2=f2, bank=bank: e.scalar_tensor_tensor(
                    out=IL[:, f2, :], in0=bank[:, :], scalar=0.0, in1=f(IH[:, f2, :]), op0=ALU.max,
                    op1=ALU.subtract), th, last.get("ih"))
                rel(bank, tl)
                yield 0.60
            last["x2h"] = last["ul"] = tk
            while not M.free:
                yield
            bank, free_ = M.get()
            for t in range(2):
                prs = []
                for c in range(8):
                    o = (c % 2) * 256 + t * 128
                    prs.append((IH[:, c // 2, o:o + 128], IL[:, c // 2, o:o + 128], WP[0][:, c, :], WP[1][:, c, :]))
                for i, (lh, ll, rh, rl) in enumerate(prs):
                    for j, (x, y) in enumerate(((lh, rh), (lh, rl), (ll, rh))):
                        s, e_ = (i == 0 and j == 0), (i == 7 and j == 2)
                        tk = PE.do(lambda e, x=x, y=y, s=s, e_=e_, t=t, bank=bank: e.matmul(
                            bank[:, t * 256:t * 256 + 256], x, y, start=s, stop=e_),
                            free_, th, tl, tok_w["p"], signal=(e_ and t == 1))
                    if i % 2 == 1 and not (i == 7 and t == 1):
                        yield 0.60
            last["ih"] = tk
            yield 0.40
            b3 = bank[:, :].rearrange("p (t c) -> p t c", t=2)
            ty = DVE.do(lambda e: e.tensor_tensor(X2b[:, :, :], b3, X2b[:, :, :], ALU.add), tk, tb)
            rel(bank, ty)
            yield
            tn = yield from normalise(XO, X2b, ty, out_tok.get(b - 1), "d")
            last["x2b"] = tn
            out_tok[b] = dO.dma(out[b * 256:b * 256 + 256, :].rearrange("(t p) c -> p t c", p=128),
                                       XO[:, :, :], tn)
            yield

        def merge(gens):
            live = [[start, g] for g, start in gens]
            while live:
                x = min(live, key=lambda v: v[0])
                try:
                    x[0] += next(x[1]) or 0.1
                except StopIteration:
                    live.remove(x)

        gens = [(attention(), 0), (weights(), -31)]
        for b in range(NB):
            gens.append((stage1(b), 16 * b + S1))
            gens.append((stage2a(b), 16 * b + S2A))
            gens.append((stage2c(b), 16 * b + S2C))
            gens.append((stage3(b), 16 * b + S3))
        merge(gens)
        SP.wait(out_tok[NB - 1])

        block = ctx.enter_context(nc.Block())

        @block.sync
        def _(eng):
            SP.run(eng)

        @block.gpsimd
        def _(eng):
            POOL.run(eng)

        @block.scalar
        def _(eng):
            ACTE.run(eng)

        @block.vector
        def _(eng):
            DVE.run(eng)

        @block.tensor
        def _(eng):
            PE.run(eng)


def kernel(**inputs):
    import numpy as np
    import concourse.bacc as bacc
    from concourse import mybir as mb
    from concourse.bass_utils import run_bass_kernel_spmd as run

    i = {k: np.asarray(v) for k, v in inputs.items()}
    fr = i["fside_BxS2_0"]
    arrays = {
        "x": i["x"].reshape(4096, 256),
        "ctxT": i["ctx_1024"].reshape(4096, 256).T,
        "frac": fr,
        "fT": fr.reshape(32, 128).T,
        "kT": i["L0_attn_w_fc"].reshape(1024, 64).T,
        "v": i["L0_attn_w_proj"].T.reshape(1024, 64),
        "ln_g": i["L0_attn_ln_g"],
        "ln_b": i["L0_attn_ln_b"],
        "WqT": i["L0_xattn_Wq"].T,
        "WkT": i["L0_xattn_Wk"].T,
        "WvT": i["L0_xattn_Wv"].T,
        "WoT": i["L0_xattn_Wo"].T,
        "bq": i["L0_xattn_bq"].reshape(2, 128).T,
        "bk": i["L0_xattn_bk"].reshape(2, 128).T,
        "bv": i["L0_xattn_bv"].reshape(2, 128).T,
        "bo": i["L0_xattn_bo"],
        "alpha_pos": i["L0_xattn_alpha_pos"],
        "alpha_neg": i["L0_xattn_alpha_neg"],
        "gamma": i["L0_xattn_gamma"].reshape(1),
        "delta": i["L0_xattn_delta"].reshape(1),
        "gateT": i["L0_ffn_gate_W"].T,
        "gate_b": i["L0_ffn_gate_b"].reshape(8, 1),
        "wiT": i["L0_ffn_wi_W"].T,
        "wi_b": i["L0_ffn_wi_b"],
        "woT": i["L0_ffn_wo_W"].T,
        "wo_b": i["L0_ffn_wo_b"],
        "loraA": i["L0_ffn_lora_A"].reshape(32, 256).T,
        "loraB": i["L0_ffn_lora_B"].transpose(0, 2, 1).reshape(32, 1024),
    }
    arrays = {k: np.ascontiguousarray(v) for k, v in arrays.items()}
    nc = bacc.Bacc("TRN2", target_bir_lowering=False, num_devices=1)
    aps = {k: nc.dram_tensor(f"in_{k}", v.shape, mb.dt.from_np(v.dtype), kind="ExternalInput").ap()
           for k, v in arrays.items()}
    o = nc.dram_tensor("out_0", (4096, 256), mb.dt.float32, kind="ExternalOutput").ap()
    decoder_layer(nc, aps, o)
    r = run(nc, [{f"in_{k}": v for k, v in arrays.items()}], core_ids=[0])
    return r.results[0]["out_0"].reshape(16, 256, 256)
```

```python
import concourse.bass as bass
from concourse import mybir
from contextlib import ExitStack


def decoder_layer(nc, a, out):
    f32 = mybir.dt.float32
    f32r = mybir.dt.float32r
    ALU = mybir.AluOpType
    ACT = mybir.ActivationFunctionType
    AX = mybir.AxisListType

    NB = 16
    EPS = 1e-5
    CLIP = 0.2
    BIG = 3.0e38
    START_W, START = -27, (-30, -12.5, 20, 28)
    SHIFT = {(1, 0): 0.5, (14, 1): -0.5, (15, 1): 2, (15, 2): -4, (15, 3): -4}

    ctx = ExitStack()
    with ctx:
        def sb(name, shape, dt=f32):
            return ctx.enter_context(nc.sbuf_tensor(name, shape, dt))

        def sem(name):
            return ctx.enter_context(nc.semaphore(name))

        class Later:

            def activation(self, *a, **k):
                return lambda e: e.activation(*a, **k)

            def affine_select(self, *a, **k):
                return lambda e: e.affine_select(*a, **k)

            def bn_aggr(self, *a, **k):
                return lambda e: e.bn_aggr(*a, **k)

            def bn_stats(self, *a, **k):
                return lambda e: e.bn_stats(*a, **k)

            def dma_start(self, *a, **k):
                return lambda e: e.dma_start(*a, **k)

            def matmul(self, *a, **k):
                return lambda e: e.matmul(*a, **k)

            def memset(self, *a, **k):
                return lambda e: e.memset(*a, **k)

            def reciprocal(self, *a, **k):
                return lambda e: e.reciprocal(*a, **k)

            def scalar_tensor_tensor(self, *a, **k):
                return lambda e: e.scalar_tensor_tensor(*a, **k)

            def tensor_reduce(self, *a, **k):
                return lambda e: e.tensor_reduce(*a, **k)

            def tensor_scalar(self, *a, **k):
                return lambda e: e.tensor_scalar(*a, **k)

            def tensor_tensor(self, *a, **k):
                return lambda e: e.tensor_tensor(*a, **k)

            def tensor_tensor_reduce(self, *a, **k):
                return lambda e: e.tensor_tensor_reduce(*a, **k)

            def transpose(self, *a, **k):
                return lambda e: e.transpose(*a, **k)

        later = Later()

        class Lane:

            def __init__(self, name):
                self.name, self.sem, self.n, self.queue, self.seen = name, sem("s_" + name), 0, [], {}

            def wait(self, *tokens):
                for t in tokens:
                    if type(t) is list:
                        self.wait(*t)
                    elif t is not None and self.seen.get(t[0].name, 0) < t[1]:
                        self.seen[t[0].name] = t[1]
                        self.queue.append((t[0], t[1], None))

            def do(self, fn, *tokens, signal=True):
                self.wait(*tokens)
                fn = fn(later)
                if not signal:
                    self.queue.append((None, 0, fn))
                    return None
                self.n += 1
                self.queue.append((self.sem, 1, fn))
                return (self.sem, self.n)

            def run(self, eng):
                for s, v, fn in self.queue:
                    if fn is None:
                        eng.wait_ge(s, v)
                    elif s is None:
                        fn(eng)
                    else:
                        fn(eng).then_inc(s, v)

        PE, ACTE, DVE, POOL, SP = (Lane(n) for n in ("pe", "act", "dve", "pool", "sp"))

        class Stream:

            def __init__(self, name):
                self.sem, self.n = sem("d_" + name), 0

            def dma(self, dst, src, *tokens):
                SP.wait(*tokens)
                self.n += 16
                SP.queue.append((self.sem, 16, lambda e: e.dma_start(dst, src)))
                return (self.sem, self.n)

        psum = [ctx.enter_context(nc.psum_tensor(f"bank{i}", [128, 512], f32)) for i in range(8)]
        pL, pT, pV, pA = psum[3:5], psum[5], psum[6], psum[7]

        class Banks:

            def __init__(self):
                self.free = [(psum[i], None) for i in range(3)]

            def get(self):
                return self.free.pop(0)

            def put(self, bank, token):
                self.free.append((bank, token))

        M = Banks()

        ident = sb("ident", [128, 128])
        KH, KL = sb("KH", [128, 1024], f32r), sb("KL", [128, 1024], f32r)
        VS = sb("VS", [128, 8, 64])
        W = {}
        for n in ("q", "k", "v", "o"):
            W[n] = (sb(f"W{n}h", [128, 2, 256], f32r), sb(f"W{n}l", [128, 2, 256], f32r))
        WI = (sb("WIh", [128, 2, 1024], f32r), sb("WIl", [128, 2, 1024], f32r))
        WP = (sb("WPh", [128, 8, 256], f32r), sb("WPl", [128, 8, 256], f32r))
        GA = (sb("GAh", [128, 2, 40], f32r), sb("GAl", [128, 2, 40], f32r))
        LB = sb("LB", [128, 1024], f32r)
        gB, bB = sb("gB", [128, 256]), sb("bB", [128, 256])
        boB, woB = sb("boB", [128, 256]), sb("woB", [128, 256])
        bqk = sb("bqk", [128, 4])
        bvc = sb("bvc", [128, 2])
        gate_b = sb("gate_b", [40, 1])
        fT = sb("fT", [128, 32])
        alph = sb("alph", [128, 32])
        gd = sb("gd", [128, 2])
        mhalf = sb("mhalf", [128, 2])
        dec8 = sb("dec8", [128, 8])

        NX = 2
        XG = [sb(f"XG{i}", [128, 2, 256]) for i in range(NX)]
        XN = sb("XN", [128, 2, 256])
        SK = sb("SK", [128, 2, 2, 256], f32r)
        NR = 6
        R = [sb(f"R{i}", [128, 512]) for i in range(NR)]
        OT = sb("OT", [128, 2, 256])
        X1 = sb("X1", [128, 2, 256])
        X1b = [sb(f"X1b{i}", [128, 2, 256]) for i in range(2)]
        X1H, X1L = sb("X1H", [128, 2, 256], f32r), sb("X1L", [128, 2, 256], f32r)
        CT = sb("CT", [128, 2, 256])
        CH, CL = sb("CH", [128, 2, 256], f32r), sb("CL", [128, 2, 256], f32r)
        QK = sb("QK", [128, 4, 2, 256], f32r)
        NS = 2
        QS = [sb(f"QS{i}", [128, 2, 4, 256], f32r) for i in range(NS)]
        VV = [sb(f"VV{i}", [128, 2, 16, 32]) for i in range(2)]
        FK = sb("FK", [128, 256])
        dp, dn = sb("DP", [128, 512]), sb("DN", [128, 512])
        NU, NT, NP, NQ = 2, 3, 3, 6
        U = [sb(f"U{i}", [128, 512]) for i in range(NU)]
        T = [sb(f"T{i}", [128, 512]) for i in range(NT)]
        NM = sb("NM", [128, 8, 2])
        P = [sb(f"P{i}", [128, 512]) for i in range(NP)]
        STG = sb("STG", [128, NQ, 512])
        PT = [STG[:, i, :] for i in range(NQ)]
        OV = [sb(f"OV{i}", [128, 2, 256]) for i in range(2)]
        RC = sb("RC", [128, 2, 16])
        AO = sb("AO", [128, 2, 256])
        X2 = sb("X2", [128, 2, 256])
        X2b = sb("X2b", [128, 2, 256])
        X2H, X2L = sb("X2H", [128, 2, 256], f32r), sb("X2L", [128, 2, 256], f32r)
        GS = sb("GS", [40, 256])
        g1, g2 = sb("g1", [128, 2, 8]), sb("g2", [128, 2, 8])
        gm = sb("gm", [128, 4])
        U2 = sb("U2", [128, 2, 32])
        UL = sb("UL", [128, 256], f32r)
        IH, IL = sb("IH", [128, 4, 512], f32r), sb("IL", [128, 4, 512], f32r)
        XO = sb("XO", [128, 2, 256])
        SM = {k: sb("SM" + k, [128, 24]) for k in "abcd"}

        def f(ap):
            return ap.bitcast(f32)

        def split(hi, lo, src, src_tok, hi_free, lo_free):
            th = ACTE.do(lambda e: e.activation(hi, src, ACT.Copy), src_tok, hi_free)
            tl = DVE.do(lambda e: e.tensor_tensor(lo, src, f(hi), ALU.subtract), th, src_tok, lo_free)
            return th, tl

        def normalise(dst, src, src_tok, dst_free, k):
            s = SM[k]
            st = s[:, 0:12].rearrange("p (t c) -> p t c", t=2)
            mv = s[:, 12:16].rearrange("p (t c) -> p t c", t=2)
            for t in range(2):
                tk = DVE.do(lambda e, t=t: e.bn_stats(st[:, t, :], src[:, t, :]), src_tok)
            for t in range(2):
                tk = DVE.do(lambda e, t=t: e.bn_aggr(mv[:, t, :], st[:, t, :]), tk)
            tk = DVE.do(lambda e: e.tensor_scalar(s[:, 16:18], mv[:, :, 1], EPS, None, ALU.add), tk)
            yield 0.55
            tk = POOL.do(lambda e: e.tensor_tensor(s[:, 18:20], s[:, 16:18], mhalf[:, :], ALU.pow), tk, tok_mh)
            yield 1.00
            if k in "bc":
                tk = DVE.do(lambda e: e.scalar_tensor_tensor(out=s[:, 20:22], in0=mv[:, :, 0], scalar=-1.0,
                                                             in1=s[:, 18:20], op0=ALU.mult, op1=ALU.mult), tk)
                yield 0.10
                for t in range(2):
                    last = ACTE.do(lambda e: e.activation(dst[:, t, :], src[:, t, :], ACT.Identity,
                                                          bias=s[:, 20 + t:21 + t], scale=s[:, 18 + t:19 + t]),
                                   tk, dst_free)
                return last
            for t in range(2):
                last = DVE.do(lambda e, t=t: e.tensor_scalar(dst[:, t, :], src[:, t, :], mv[:, t, 0:1],
                                                             s[:, 18 + t:19 + t], ALU.subtract, ALU.mult),
                              tk, dst_free)
            return last

        def transposed(src, src_tok, hi, lo, hi_free, lo_free):
            while not M.free:
                yield
            bank, free = M.get()
            for m in range(2):
                for t in range(2):
                    tk = PE.do(lambda e, m=m, t=t: e.transpose(
                        bank[:, m * 256 + t * 128:m * 256 + t * 128 + 128],
                        src[:, t, m * 128:m * 128 + 128], ident[:, :]), src_tok, free, signal=(m + t == 2))
            b3 = bank[:, :].rearrange("p (m t) -> p m t", m=2)
            yield 0.30
            th = ACTE.do(lambda e: e.activation(hi, b3, ACT.Copy), tk, hi_free)
            yield 0.30
            tl = DVE.do(lambda e: e.tensor_tensor(lo, b3, f(hi), ALU.subtract), th, lo_free)
            M.put(bank, tl)
            yield 0.35
            return th, tl

        def mm3(bank_ap, pairs, tokens, signal):
            n = len(pairs)
            tk = None
            for i, (lh, ll, rh, rl) in enumerate(pairs):
                for j, (x, y) in enumerate(((lh, rh), (lh, rl), (ll, rh))):
                    s, e_ = (i == 0 and j == 0), (i == n - 1 and j == 2)
                    tk = PE.do(lambda e, x=x, y=y, s=s, e_=e_: e.matmul(bank_ap, x, y, start=s, stop=e_),
                               *tokens, signal=signal and e_)
            return tk

        last = {}
        done = set()

        dS, dG, dK = Stream("small"), Stream("ln"), Stream("k")
        tk = POOL.do(lambda e: e.memset(ident[:, :], 0.0))
        tok_id = POOL.do(lambda e: e.affine_select(out=ident[:, :], in_=ident[:, :], compare_op=ALU.not_equal,
                                                   fill=1.0, base=0, pattern=[[-1, 128]],
                                                   channel_multiplier=1), tk)
        tok_mh = POOL.do(lambda e: e.memset(mhalf[:, :], -0.5))

        dX, dC, dF = [Stream(f"x{i}") for i in range(NX)], Stream("c"), Stream("f")

        def load_x(b, free):
            return dX[b % NX].dma(XG[b % NX][:, :, :],
                                 a["x"][b * 256:b * 256 + 256, :].rearrange("(t p) c -> p t c", p=128), free)

        def load_c(b, free):
            return dC.dma(CT[:, :, :],
                                 a["ctxT"][:, b * 256:b * 256 + 256].rearrange("(k p) t -> p k t", p=128), free)

        def load_f(b, free):
            return dF.dma(FK[:, :], a["frac"][b, :].partition_broadcast(128), free)

        xl, cl, fl = {0: load_x(0, None)}, {}, {}

        def stage(n_cols, slot):
            return STG[:, slot:slot + (n_cols + 511) // 512, :].rearrange("p a b -> p (a b)")[:, 0:n_cols]

        dW = [Stream(f"w{i}") for i in range(3)]
        reg = [(0, 2), (2, 2), (4, 2)]
        free = [None, None, None]

        def weight(i, src_ap, parts, shape, hi, lo, scale=None, scale_tok=None):
            st = stage(shape[0] * shape[1], reg[i][0])[0:parts, :]
            v = st.rearrange("p (a b) -> p a b", a=shape[0])
            tk = dW[i].dma(v, src_ap, free[i])
            if scale is not None:
                tk = DVE.do(lambda e: e.tensor_scalar(v, v, scale[0:parts, :], 0.25, ALU.mult, ALU.mult),
                            tk, scale_tok)
            th, tl = split(hi, lo, v, tk, None, None)
            free[i] = tl
            return tl

        st = stage(1024, 0)
        dW[0].dma(st[0:64, :], a["kT"])
        tk = dW[0].dma(st[64:128, :], a["kT"])
        dG.dma(gB[:, :], a["ln_g"].partition_broadcast(128))
        tok_g = dG.dma(bB[:, :], a["ln_b"].partition_broadcast(128))
        tok_vs = dK.dma(VS[:, :, :], a["v"].rearrange("(c p) d -> p c d", p=128))
        tok_kh, tok_k = split(KH[:, :], KL[:, :], st, tk, None, None)
        free[0] = tok_k
        tok_s = {}

        def col(src, k):
            return src.rearrange("(k p) e -> p k e", p=128)

        tok_w = {}

        def weights():
            dS.dma(boB[:, :], a["bo"].partition_broadcast(128))
            dS.dma(woB[:, :], a["wo_b"].partition_broadcast(128))
            dS.dma(alph[:, 0:16], a["alpha_pos"].partition_broadcast(128))
            dS.dma(alph[:, 16:32], a["alpha_neg"].partition_broadcast(128))
            dS.dma(gd[:, 0:1], a["gamma"].partition_broadcast(128))
            dS.dma(gd[:, 1:2], a["delta"].partition_broadcast(128))
            dS.dma(bqk[:, 0:2], a["bq"])
            dS.dma(bqk[:, 2:4], a["bk"])
            dS.dma(bvc[:, :], a["bv"])
            tok_s["small"] = dS.dma(fT[:, :], a["fT"])
            yield 0.11
            t = POOL.do(lambda e: e.memset(gate_b[:, :], 0.0))
            for i in range(8):
                t = POOL.do(lambda e: e.memset(dec8[:, i:i + 1], float(8 - i)), t)
            t = POOL.do(lambda e: e.memset(f(UL[96:128, :]), 1.0), t)
            tok_lbz = POOL.do(lambda e: e.memset(f(LB[96:128, :]), 0.0), t)
            t = tok_lbz
            for i in range(2):
                t = POOL.do(lambda e: e.memset(VV[i][:, :, :, 16:32], 0.0), t)
                t = POOL.do(lambda e: e.memset(VV[i][:, :, :, 16:17], 1.0), t)
            tok_c = tok_s["c"] = t
            yield 0.50
            t1 = DVE.do(lambda e: e.tensor_scalar(bqk[:, 0:2], bqk[:, 0:2], gd[:, 0:1], 0.25, ALU.mult, ALU.mult),
                        (dS.sem, dS.n))
            t2 = DVE.do(lambda e: e.tensor_scalar(alph[:, :], alph[:, :], gd[:, 1:2], None, ALU.mult))
            tok_w["small"] = t2
            tok_w["v"] = weight(1, col(a["WvT"], 2), 128, (2, 256), W["v"][0][:, :, :], W["v"][1][:, :, :])
            yield 0.90
            tok_w["k"] = weight(2, col(a["WkT"], 2), 128, (2, 256), W["k"][0][:, :, :], W["k"][1][:, :, :])
            yield 1.40
            tok_w["q"] = weight(0, col(a["WqT"], 2), 128, (2, 256), W["q"][0][:, :, :], W["q"][1][:, :, :],
                                gd[:, 0:1], (dS.sem, dS.n))
            yield 0.65
            for t in QS:
                for i in range(2):
                    tok_s["zero"] = POOL.do(lambda e: e.memset(f(t[:, i, :, :]), 0.0))
                    yield 0.30
            st = stage(512, reg[1][0])
            v = st.rearrange("p (a b) -> p a b", a=2)
            tk = dW[1].dma(v, col(a["WoT"], 2), free[1])
            th, tl = split(W["o"][0][:, :, :], W["o"][1][:, :, :], v, tk, None, None)
            while not M.free:
                yield
            bank, bf = M.get()
            for k in range(2):
                tp = PE.do(lambda e, k=k: e.matmul(bank[:, 0:256], bvc[:, k:k + 1].to_broadcast([128, 128]),
                                                   v[:, k, :], start=(k == 0), stop=(k == 1)),
                           bf, tk, (dS.sem, dS.n), signal=(k == 1))
            t3 = DVE.do(lambda e: e.tensor_tensor(boB[:, :], boB[:, :], bank[:, 0:256], ALU.add), tp)
            M.put(bank, t3)
            free[1] = t3
            tok_w["o"] = t3
            yield 1.00
            for h in range(2):
                tok_w["i"] = weight(2 * h, a["wiT"][h * 128:h * 128 + 128, :].rearrange("p (a e) -> p a e", a=1),
                                    128, (1, 1024), WI[0][:, h:h + 1, :], WI[1][:, h:h + 1, :])
                yield 0.95
            for h in range(2):
                tok_w["p"] = weight(1 + h, a["woT"][h * 512:h * 512 + 512, :].rearrange("(k p) e -> p k e", p=128),
                                    128, (4, 256), WP[0][:, 4 * h:4 * h + 4, :], WP[1][:, 4 * h:4 * h + 4, :])
                yield 1.45
            st = stage(80, reg[0][0])
            v = st.rearrange("p (a b) -> p a b", a=2)
            dW[0].dma(v[:, :, 0:32], col(a["loraA"], 2), free[0])
            tk = dW[0].dma(v[:, :, 32:40], col(a["gateT"], 2))
            th, tl = split(GA[0][:, :, :], GA[1][:, :, :], v, tk, None, None)
            free[0] = tl
            tok_w["g"] = dS.dma(gate_b[32:40, :], a["gate_b"], tok_c)
            yield 1.05
            st = stage(1024, reg[1][0])
            for r in range(3):
                tk = dW[1].dma(st[32 * r:32 * r + 32, :], a["loraB"], free[1])
            th = ACTE.do(lambda e: e.activation(LB[0:96, :], st[0:96, :], ACT.Copy), tk)
            tl = DVE.do(lambda e: e.tensor_tensor(LB[64:96, :], st[64:96, :], f(LB[64:96, :]), ALU.subtract), th)
            bh, bl = IH[0:1, 0:2, :], IL[0:1, 0:2, :]
            st2 = stage(1024, reg[2][0])[0:1, :].rearrange("p (a b) -> p a b", a=2)
            tk = dW[2].dma(st2, a["wi_b"].rearrange("(o a b) -> o a b", o=1, a=2), free[2])
            th2, tl2 = split(bh, bl, st2, tk, None, None)
            t4 = dW[1].dma(f(LB[96:97, :]).rearrange("p (a b) -> p a b", a=2), f(bh), th2, tl2, tok_lbz)
            t4 = dW[1].dma(f(LB[97:98, :]).rearrange("p (a b) -> p a b", a=2), f(bl))
            tok_w["lb"] = (th, tl, t4)
            free[1] = free[2] = tl
            tok_w["stage"] = [tl, tl2, tok_w["g"]]
            yield 0.75

        x1_tok, x1t_tok = {}, {}

        def stage1(b):
            xg = XG[b % NX]
            if b == 0:
                cl[0], fl[0] = load_c(0, None), load_f(0, None)
            tx = yield from normalise(XN, xg, xl[b], last.get("xn"), "a")
            gb = gB[:, :].unsqueeze(1).to_broadcast([128, 2, 256])
            bb = bB[:, :].unsqueeze(1).to_broadcast([128, 2, 256])
            lane = POOL if b else DVE
            tx = lane.do(lambda e: e.tensor_tensor(XN[:, :, :], XN[:, :, :], gb, ALU.mult), tx, tok_g)
            tx = lane.do(lambda e: e.tensor_tensor(XN[:, :, :], XN[:, :, :], bb, ALU.add), tx)
            yield 0.85
            while b > 0 and ("1", b - 1) not in done:
                yield 0.01
            if b + 1 < NB:
                xl[b + 1] = load_x(b + 1, last.get(("y1", b + 1 - NX)))
            while not M.free:
                yield
            bank, free_ = M.get()
            for hp in range(2):
                for t in range(2):
                    tk = PE.do(lambda e, hp=hp, t=t, bank=bank: e.transpose(
                        bank[:, hp * 256 + t * 128:hp * 256 + t * 128 + 128],
                        XN[:, t, hp * 128:hp * 128 + 128], ident[:, :]),
                        tx, free_, tok_id, signal=(hp + t == 2))
            last["xn"] = tk
            b3 = bank[:, :].rearrange("p (h t) -> p h t", h=2)
            yield 0.25
            for h in range(2):
                own, other = slice(64 * h, 64 * h + 64), slice(64 - 64 * h, 128 - 64 * h)
                th = ACTE.do(lambda e, h=h, own=own, b3=b3: e.activation(SK[own, :, h, :], b3[own, :, :], ACT.Copy),
                             tk, last.get("sk"))
            yield 0.70
            for h in range(2):
                own, other = slice(64 * h, 64 * h + 64), slice(64 - 64 * h, 128 - 64 * h)
                tl = DVE.do(lambda e, h=h, own=own, other=other, b3=b3: e.tensor_tensor(
                    SK[other, :, h, :], b3[own, :, :], f(SK[own, :, h, :]), ALU.subtract), th)
            M.put(bank, tl)
            sk_tok = [th, tl]
            yield 0.40
            units = [(hp, c2, h) for hp in range(2) for c2 in range(4) for h in range(2)]
            sq = {}

            def av(j):
                hp, c2, _ = units[2 * j]
                for i in range(2):
                    for h in range(2):
                        r, ts = sq[2 * j + h]
                        c = 2 * c2 + i
                        tk = PE.do(lambda e, r=r, i=i, h=h, c=c, hp=hp: e.matmul(
                            pA[64 * h:64 * h + 64, hp * 256:hp * 256 + 256], VS[:, c, :],
                            r[:, i * 256:i * 256 + 256], start=(c == 0), stop=(c == 7),
                            skip_group_check=True),
                            ts, tok_vs, last.get("pA"), signal=(i == 1 and h == 1))
                for h in range(2):
                    last[("r", (last["rn"][2 * j + h]))] = tk
                return tk

            last["rn"], held = {}, {}

            def scores(u):
                hp, c2, h = units[u]
                bank, free_ = M.get()
                for i in range(2):
                    c = 2 * c2 + i
                    for n, kk in enumerate((KH, KL)):
                        tk = PE.do(lambda e: e.matmul(
                            bank[:, i * 256:i * 256 + 256], kk[:, c * 128:c * 128 + 128], SK[:, hp, h, :],
                            start=(n == 0), stop=(n == 1)),
                            free_, sk_tok, tok_kh, tok_k, signal=(i == 1 and n == 1))
                last["sk"] = tk
                held[u] = (bank, tk)

            def relu(u):
                bank, tk = held[u]
                slot = (b * 16 + u) % NR
                last["rn"][u] = slot
                tr = ACTE.do(lambda e: e.activation(R[slot][:, :], bank[:, :], ACT.Relu), tk, last.get(("r", slot)))
                M.put(bank, tr)
                held[u] = (R[slot], tr)

            def square(u):
                r, tr = held[u]
                lane = DVE if u % 8 == 7 or b < 2 and u % 2 else POOL
                sq[u] = (r, lane.do(lambda e: e.tensor_tensor(r[:, :], r[:, :], r[:, :], ALU.mult), tr))

            for u in range(18):
                if u < 16:
                    while not M.free:
                        yield 0.11
                    scores(u)
                yield 0.10
                if 1 <= u < 17:
                    relu(u - 1)
                yield 0.10
                if u >= 2:
                    square(u - 2)
                yield 0.05
                if u % 2 == 1 and u >= 5:
                    av((u - 5) // 2)
                yield 0.30
            yield 0.01
            tk = av(7)
            yield 0.01
            src = pA[:, :].rearrange("p (h t) -> p h t", h=2)
            to = ACTE.do(lambda e: e.activation(OT[:, :, :], src, ACT.Copy), tk, last.get("ot"))
            last["pA"] = to
            yield 0.30
            while not M.free:
                yield
            bank, free_ = M.get()
            for t in range(2):
                for hp in range(2):
                    tk = PE.do(lambda e, t=t, hp=hp: e.transpose(
                        bank[:, t * 256 + hp * 128:t * 256 + hp * 128 + 128],
                        OT[:, hp, t * 128:t * 128 + 128], ident[:, :]), to, free_, signal=(t + hp == 2))
            last["ot"] = tk
            yield 0.35
            b3 = bank[:, :].rearrange("p (t c) -> p t c", t=2)
            ty = DVE.do(lambda e: e.scalar_tensor_tensor(out=xg[:, :, :], in0=xg[:, :, :], scalar=2.0, in1=b3,
                                                         op0=ALU.mult, op1=ALU.add), tk)
            M.put(bank, ty)
            yield 0.11
            x1_tok[b] = yield from normalise(X1, xg, ty, last.get("x1"), "b")
            last[("y1", b)] = x1_tok[b]
            done.add(("1", b))
            yield 0.05

        dQ = [Stream(f"q{i}") for i in range(NS)]
        x2_tok = {}

        tok_d, tok_v, st_tok, qk_free = {}, {}, {}, {-1: None}
        tlg, tu, tlog, texp, tturn, tev = {}, {}, {}, {}, {}, {}

        def differences(b):
            for q in range(2):
                td = DVE.do(lambda e, q=q: e.tensor_scalar(dn[:, q * 256:q * 256 + 256], FK[:, :],
                                                           fT[:, 2 * b + q:2 * b + q + 1], CLIP,
                                                           ALU.subtract, ALU.min), fl[b], tlog.get(16 * b - 1))
            if b + 1 < NB:
                fl[b + 1] = load_f(b + 1, td)
            tdp = DVE.do(lambda e: e.tensor_scalar(dp[:, :], dn[:, :], 0.0, None, ALU.max), td)
            tdn = DVE.do(lambda e: e.tensor_scalar(dn[:, :], dn[:, :], -CLIP, 0.0, ALU.max, ALU.min), tdp)
            tok_d[b] = (tdp, tdn)

        def stage2a(b):
            while b not in x1_tok or (b >= 2 and ("2c", b - 2) not in done):
                yield
            th = ACTE.do(lambda e: e.activation(CH[:, :, :], CT[:, :, :], ACT.Copy), cl[b], last.get("ch"))
            yield 0.60
            tl = DVE.do(lambda e: e.tensor_tensor(CL[:, :, :], CT[:, :, :], f(CH[:, :, :]), ALU.subtract),
                        th, last.get("ch"))
            if b + 1 < NB:
                cl[b + 1] = load_c(b + 1, tl)
            yield 0.10
            xh, xlo = yield from transposed(X1, x1_tok[b], X1H[:, :, :], X1L[:, :, :],
                                            last.get("x1h"), last.get("x1h"))
            tx1b = POOL.do(lambda e: e.tensor_tensor(X1b[b % 2][:, :, :], X1[:, :, :],
                                                     boB[:, :].unsqueeze(1).to_broadcast([128, 2, 256]), ALU.add),
                           x1_tok[b], tok_w["o"], last.get(("x1b", b - 2)))
            last["x1"] = [xh, tx1b]
            last[("tx1b", b)] = tx1b
            yield 0.20

            def project(n, src, toks, bias, hi, lo, key):
                while not M.free:
                    yield
                bank, free_ = M.get()
                wh, wl = W[n]
                for m in range(2):
                    cs = slice(m * 128, m * 128 + 128)
                    tk = mm3(bank[:, m * 256:m * 256 + 256],
                             [(wh[:, k, cs], wl[:, k, cs], src[0][:, k, :], src[1][:, k, :]) for k in range(2)],
                             [free_, tok_w[n], *toks], m == 1)
                yield 0.45
                for m in range(2):
                    bm = bank[:, m * 256:m * 256 + 256]
                    th = ACTE.do(lambda e, m=m, bm=bm: e.activation(hi[:, m, :], bm, ACT.Identity,
                                                                    bias=bqk[:, bias + m:bias + m + 1]),
                                 tk, last.get(key), tok_w["small"])
                yield 0.30
                for m in range(2):
                    bm = bank[:, m * 256:m * 256 + 256]
                    tl = DVE.do(lambda e, m=m, bm=bm: e.scalar_tensor_tensor(
                        out=lo[:, m, :], in0=bm, scalar=bqk[:, bias + m:bias + m + 1], in1=f(hi[:, m, :]),
                        op0=ALU.add, op1=ALU.subtract), th, last.get(key))
                M.put(bank, tl)
                return th, tl, tk

            while b - 1 not in qk_free:
                yield
            kt = yield from project("k", (CH, CL), (th, tl), 2, QK[:, 2], QK[:, 3], "qk")
            yield 0.10
            qt = yield from project("q", (X1H, X1L), (xh, xlo), 0, QK[:, 1], QK[:, 0], "qk")
            last["x1h"] = qt[2]
            made[b] = [kt[0], kt[1], qt[0], qt[1]]
            yield 0.50
            while not M.free:
                yield
            bank, free_ = M.get()
            wh, wl = W["v"]
            for t in range(2):
                ts_ = slice(t * 128, t * 128 + 128)
                tk = mm3(bank[:, t * 256:t * 256 + 256],
                         [(CH[:, k, ts_], CL[:, k, ts_], wh[:, k, :], wl[:, k, :]) for k in range(2)],
                         [free_, tok_w["v"], th, tl], t == 1)
            last["ch"] = tk
            yield 0.20
            for t in range(2):
                tv = ACTE.do(lambda e, t=t: e.activation(
                    VV[b % 2][:, t, :, 0:16], bank[:, t * 256:t * 256 + 256].rearrange("p (h d) -> p h d", h=16),
                    ACT.Copy),
                    tk, last.get(("pt", 16 * (b - 1) - 1)), tok_s["c"])
            M.put(bank, tv)
            tok_v[b] = tv
            done.add(("2a", b))
            yield 0.10

        made = {}

        def restack(G):
            b, g = G // 4, G % 4
            s = G % NS
            for r, (q, k) in enumerate(((1, 2), (0, 2), (1, 3))):
                for j in range(2):
                    p = 32 * g + 16 * j
                    dst, src = QS[s][16 * r:16 * r + 16, :, 2 * j:2 * j + 2, :], QK[p:p + 16, q:k + 1:k - q, :, :]
                    tk = dQ[s].dma(f(dst).rearrange("p a m t -> p a (m t)"), f(src).rearrange("p a m t -> p a (m t)"),
                                   *made[b], last.get(("qs", s)), tok_s["zero"])
            st_tok[G] = tk
            if g == 3:
                last["qk"] = tk
                qk_free[b] = tk

        def head(n):
            return (n % 16) // 2 + 8 * (n % 2)

        def logits(n):
            b, h = n // 16, head(n)
            tdp = tok_d[b][0]
            s, L = (n // 4) % NS, pL[n % 2]
            for q in range(2):
                tk = PE.do(lambda e, q=q: e.matmul(L[:, q * 256:q * 256 + 256],
                                                   QS[s][:, 0, n % 4, q * 128:q * 128 + 128],
                                                   QS[s][:, 1, n % 4, :],
                                                   start=True, stop=True),
                           st_tok[n // 4], last.get(("L", n - 2)), signal=(q == 1))
            last[("qs", s)] = tk
            tlg[n] = tk
            u = U[n % NU]
            tu[n] = POOL.do(lambda e: e.tensor_scalar(u[:, :], dp[:, :], alph[:, h:h + 1], 0.0, ALU.mult, ALU.add),
                            tdp, last.get(("u", n - NU)), tok_w["small"])

        def biased(n):
            h, L, u, t = head(n), pL[n % 2], U[n % NU], T[n % NT]
            t1 = DVE.do(lambda e: e.scalar_tensor_tensor(out=t[:, :], in0=dn[:, :],
                                                         scalar=alph[:, 16 + h:17 + h], in1=L[:, :],
                                                         op0=ALU.mult, op1=ALU.add),
                        tlg[n], tok_d[n // 16][1], last.get(("t", n - NT)))
            last[("L", n)] = t1
            for q in range(2):
                cs = slice(q * 256, q * 256 + 256)
                t2 = DVE.do(lambda e, q=q, cs=cs: e.tensor_tensor_reduce(
                    out=t[:, cs], in0=t[:, cs], in1=u[:, cs], scale=-1.0, scalar=BIG, op0=ALU.add,
                    op1=ALU.min, accum_out=NM[:, n % 8, q:q + 1]), t1, tu[n], last.get(("t", n - 8)))
            last[("u", n)] = t2
            tlog[n] = t2

        def exps(n):
            t, p = T[n % NT], P[n % NP]
            for q in range(2):
                cs = slice(q * 256, q * 256 + 256)
                tk = ACTE.do(lambda e, q=q, cs=cs: e.activation(p[:, cs], t[:, cs], ACT.Exp,
                                                                bias=NM[:, n % 8, q:q + 1], scale=-1.0),
                             tlog[n], last.get(("p", n - NP)))
            last[("t", n)] = tk
            texp[n] = tk

        def turn(n):
            p = P[n % NP]
            for k in range(2):
                for q in range(2):
                    tk = PE.do(lambda e, k=k, q=q: e.transpose(
                        pT[:, k * 256 + q * 128:k * 256 + q * 128 + 128],
                        p[:, q * 256 + k * 128:q * 256 + k * 128 + 128], ident[:, :]),
                        texp[n], last.get("pT"), signal=(k + q == 2))
            last[("p", n)] = tturn[n] = tk

        def turned(n):
            pt, tk = PT[n % NQ], tturn[n]
            extra = tok_w["stage"] if n < NQ else ()
            tev[n] = ACTE.do(lambda e: e.activation(pt, pT[:, :], ACT.Copy), tk, last.get(("pt", n - NQ)),
                             *extra)
            last["pT"] = tev[n]

        def values(G):
            b, g = G // 4, G % 4
            c0 = (g % 2) * 256
            for k in range(2):
                for j in range(4):
                    n = 4 * G + j
                    tk = PE.do(lambda e, k=k, j=j, n=n: e.matmul(
                        pV[32 * j:32 * j + 32, c0:c0 + 256], VV[b % 2][:, k, head(n), :],
                        PT[n % NQ][:, k * 256:k * 256 + 256],
                        start=(k == 0), stop=(k == 1), skip_group_check=True),
                        tev[n], tok_v[b], last.get("pV"), signal=(k == 1 and j == 3))
            for j in range(4):
                last[("pt", 4 * G + j)] = tk
            if g % 2:
                ov = OV[g // 2]
                to = ACTE.do(lambda e: e.activation(ov[:, :, :], pV[:, :].rearrange("p (g t) -> p g t", g=2),
                                                    ACT.Copy), tk, last.get("ov"))
                last["pV"] = to
                last[("ovt", b, g // 2)] = to

        def attention():
            N = NB * 16
            for n in range(N + 5):
                if n < N:
                    if n % 4 == 0 and n // 4 + 1 < NB * 4:
                        while n == 0 and 0 not in made:
                            yield 0.01
                        if n == 0:
                            restack(0)
                        while (n // 4 + 1) // 4 not in made:
                            yield 0.40
                        restack(n // 4 + 1)
                    if n % 16 == 0:
                        while ("2a", n // 16) not in done:
                            yield 0.36
                        if n:
                            biased(n - 1)
                        differences(n // 16)
                    logits(n)
                yield 0.20
                if 1 <= n <= N and (n % 16 or n == N):
                    biased(n - 1)
                yield 0.20
                if 3 <= n < N + 3:
                    turn(n - 3)
                yield 0.20
                if 2 <= n < N + 2:
                    exps(n - 2)
                yield 0.20
                if 3 <= n < N + 3:
                    turned(n - 3)
                if n >= 4 and (n - 4) % 4 == 3:
                    values((n - 4) // 4)
                yield 0.20

        def stage2c(b):
            while ("ovt", b, 1) not in last or (b + 1 < NB and ("2a", b + 1) not in done):
                yield
            ta = None
            for q in range(2):
                while not M.free:
                    yield
                bank, free_ = M.get()
                for g in range(4):
                    tk = PE.do(lambda e, g=g, q=q, bank=bank: e.transpose(
                        bank[:, g * 128:g * 128 + 128], OV[g // 2][:, g % 2, q * 128:q * 128 + 128], ident[:, :]),
                        last[("ovt", b, g // 2)], free_, signal=(g == 3))
                last["ov"] = tk
                yield 0.25
                v4 = bank[:, :].rearrange("p (h d) -> p h d", d=32)
                tr = DVE.do(lambda e, q=q, v4=v4: e.reciprocal(RC[:, q, :], v4[:, :, 16]), tk, last.get("ao"))
                ta = DVE.do(lambda e, q=q, v4=v4: e.tensor_tensor(
                    AO[:, q, :].rearrange("p (m h d) -> p h m d", m=2, d=16),
                    v4[:, :, 0:16].rearrange("p (h m) d -> p h m d", m=2),
                    RC[:, q, :].rearrange("p (h m) -> p h m", m=2).unsqueeze(3).to_broadcast([128, 8, 2, 16]),
                    ALU.mult), tr)
                M.put(bank, ta)
                yield 0.10
            ah, al = yield from transposed(AO, ta, CH[:, :, :], CL[:, :, :], last.get("ch"), last.get("ch"))
            last["ao"] = ah
            while not M.free:
                yield
            bank, free_ = M.get()
            wh, wl = W["o"]
            for t in range(2):
                ts_ = slice(t * 128, t * 128 + 128)
                tk = mm3(bank[:, t * 256:t * 256 + 256],
                         [(CH[:, k, ts_], CL[:, k, ts_], wh[:, k, :], wl[:, k, :]) for k in range(2)],
                         [free_, tok_w["o"], ah, al], t == 1)
            last["ch"] = tk
            yield 0.55
            b3 = bank[:, :].rearrange("p (t c) -> p t c", t=2)
            ty = DVE.do(lambda e: e.tensor_tensor(X1b[b % 2][:, :, :], b3, X1b[b % 2][:, :, :], ALU.add),
                        tk, last[("tx1b", b)])
            M.put(bank, ty)
            yield 0.05
            x2_tok[b] = yield from normalise(X2, X1b[b % 2], ty, last.get("x2"), "c")
            last[("x1b", b)] = x2_tok[b]
            done.add(("2c", b))
            yield 0.20

        dO = Stream("o")
        out_tok = {}

        def stage3(b):
            while b not in x2_tok or b > 0 and ("3h", b - 1) not in done:
                yield
            xh, xlo = yield from transposed(X2, x2_tok[b], X2H[:, :, :], X2L[:, :, :], last.get("x2h"),
                                            last.get("x2h"))
            while b > 0 and b - 1 not in out_tok:
                yield
            tb = POOL.do(lambda e: e.tensor_tensor(X2b[:, :, :], X2[:, :, :],
                                                   woB[:, :].unsqueeze(1).to_broadcast([128, 2, 256]), ALU.add),
                         x2_tok[b], tok_s["small"], last.get("x2b"))
            last["x2"] = [xh, tb]
            yield 0.10
            while not M.free:
                yield
            bank, free_ = M.get()
            tk = mm3(bank[0:40, 0:256], [(GA[0][:, k, :], GA[1][:, k, :], X2H[:, k, :], X2L[:, k, :])
                                         for k in range(2)],
                     [free_, tok_w["g"], free[0], xh, xlo], True)
            yield 0.45
            tg = ACTE.do(lambda e: e.activation(GS[:, :], bank[0:40, 0:256], ACT.Identity, bias=gate_b[:, :]),
                         tk, last.get("gs"), tok_w["g"])
            M.put(bank, tg)
            yield 0.35
            while not M.free:
                yield
            bank, free_ = M.get()
            for t in range(2):
                tk = PE.do(lambda e, t=t: e.transpose(bank[:, t * 64:t * 64 + 40], GS[:, t * 128:t * 128 + 128],
                                                      ident[0:40, 0:40]), tg, free_, signal=(t == 1))
            last["gs"] = tk
            yield 0.45
            gt = bank[:, 0:128].rearrange("p (t c) -> p t c", t=2)
            lg = gt[:, :, 32:40]

            def b8(ap):
                return ap.unsqueeze(2).to_broadcast([128, 2, 8])

            t1 = DVE.do(lambda e: e.tensor_reduce(out=gm[:, 0:2], in_=lg, op=ALU.max, axis=AX.X), tk)
            t1 = DVE.do(lambda e: e.tensor_tensor(g1[:, :, :], lg, b8(gm[:, 0:2]), ALU.is_equal), t1)
            t1 = DVE.do(lambda e: e.tensor_tensor(g1[:, :, :], g1[:, :, :],
                                                  dec8[:, :].unsqueeze(1).to_broadcast([128, 2, 8]), ALU.mult),
                        t1, tok_s["c"])
            t1 = DVE.do(lambda e: e.tensor_reduce(out=gm[:, 2:4], in_=g1[:, :, :], op=ALU.max, axis=AX.X), t1)
            t1 = DVE.do(lambda e: e.tensor_tensor(g2[:, :, :], g1[:, :, :], b8(gm[:, 2:4]), ALU.is_equal), t1)
            for t in range(2):
                t2 = DVE.do(lambda e, t=t: e.tensor_tensor(
                    U2[:, t, :].rearrange("p (e r) -> p e r", r=4),
                    gt[:, t, 0:32].rearrange("p (e r) -> p e r", r=4),
                    g2[:, t, :].unsqueeze(2).to_broadcast([128, 8, 4]), ALU.mult), t1, last.get("u2"))
            M.put(bank, t2)
            yield 0.60
            while not M.free:
                yield
            bank, free_ = M.get()
            for t in range(2):
                tk = PE.do(lambda e, t=t: e.transpose(bank[0:32, t * 128:t * 128 + 128],
                                                      U2[:, t, :],
                                                      ident[:, :]), t2, free_, signal=(t == 1))
            last["u2"] = tk
            yield 0.15
            for r in (0, 64):
                th = ACTE.do(lambda e, r=r: e.activation(UL[r:r + 32, :], bank[0:32, 0:256], ACT.Copy), tk,
                             last.get("ul"))
            yield 0.50
            tl = DVE.do(lambda e: e.tensor_tensor(UL[32:64, :], bank[0:32, 0:256], f(UL[0:32, :]),
                                                  ALU.subtract), th, last.get("ul"))
            tu_ = [th, tl]
            M.put(bank, tl)
            yield 0.70
            for f2 in range(4):
                while not M.free:
                    yield
                bank, free_ = M.get()
                for i in range(2):
                    c = 2 * f2 + i
                    cs = slice(c * 128, c * 128 + 128)
                    o = bank[:, i * 256:i * 256 + 256]
                    PE.do(lambda e, o=o, cs=cs: e.matmul(o, LB[:, cs], UL[:, :], start=True, stop=False),
                          free_, tu_, *tok_w["lb"], tok_s["c"], signal=False)
                    for k in range(2):
                        for j, (x, y) in enumerate(((WI[0], X2H), (WI[0], X2L), (WI[1], X2H))):
                            e_ = (k == 1 and j == 2)
                            tk = PE.do(lambda e, o=o, cs=cs, x=x, y=y, k=k, e_=e_: e.matmul(
                                o, x[:, k, cs], y[:, k, :], start=False, stop=e_),
                                xh, xlo, tok_w["i"], signal=(e_ and i == 1))
                th = ACTE.do(lambda e, f2=f2, bank=bank: e.activation(IH[:, f2, :], bank[:, :], ACT.Relu), tk,
                             last.get("ih"))
                yield 0.40
                tl = DVE.do(lambda e, f2=f2, bank=bank: e.scalar_tensor_tensor(
                    out=IL[:, f2, :], in0=bank[:, :], scalar=0.0, in1=f(IH[:, f2, :]), op0=ALU.max,
                    op1=ALU.subtract), th, last.get("ih"))
                M.put(bank, tl)
                yield 0.60
            last["x2h"] = last["ul"] = tk
            done.add(("3h", b))
            while not M.free:
                yield
            bank, free_ = M.get()
            for t in range(2):
                prs = []
                for c in range(8):
                    o = (c % 2) * 256 + t * 128
                    prs.append((IH[:, c // 2, o:o + 128], IL[:, c // 2, o:o + 128], WP[0][:, c, :], WP[1][:, c, :]))
                for i, (lh, ll, rh, rl) in enumerate(prs):
                    for j, (x, y) in enumerate(((lh, rh), (lh, rl), (ll, rh))):
                        s, e_ = (i == 0 and j == 0), (i == 7 and j == 2)
                        tk = PE.do(lambda e, x=x, y=y, s=s, e_=e_, t=t, bank=bank: e.matmul(
                            bank[:, t * 256:t * 256 + 256], x, y, start=s, stop=e_),
                            free_, th, tl, tok_w["p"], signal=(e_ and t == 1))
                    if i % 2 == 1 and not (i == 7 and t == 1):
                        yield 0.50
            last["ih"] = tk
            yield 0.55
            b3 = bank[:, :].rearrange("p (t c) -> p t c", t=2)
            ty = DVE.do(lambda e: e.tensor_tensor(X2b[:, :, :], b3, X2b[:, :, :], ALU.add), tk, tb)
            M.put(bank, ty)
            yield 0.01
            tn = yield from normalise(XO, X2b, ty, out_tok.get(b - 1), "d")
            last["x2b"] = tn
            out_tok[b] = dO.dma(out[b * 256:b * 256 + 256, :].rearrange("(t p) c -> p t c", p=128),
                                       XO[:, :, :], tn)
            yield 0.01

        def merge(gens):
            live = [[start, g] for g, start in gens]
            while live:
                x = min(live, key=lambda v: v[0])
                try:
                    x[0] += next(x[1]) or 0.1
                except StopIteration:
                    live.remove(x)

        gens = [(attention(), 0), (weights(), START_W)]
        for b in range(NB):
            for i, g in enumerate((stage1(b), stage2a(b), stage2c(b), stage3(b))):
                gens.append((g, 16 * b + START[i] + SHIFT.get((b, i), 0)))
        merge(gens)
        SP.wait(out_tok[NB - 1])

        block = ctx.enter_context(nc.Block())

        @block.sync
        def _(eng):
            SP.run(eng)

        @block.gpsimd
        def _(eng):
            POOL.run(eng)

        @block.scalar
        def _(eng):
            ACTE.run(eng)

        @block.vector
        def _(eng):
            DVE.run(eng)

        @block.tensor
        def _(eng):
            PE.run(eng)


def kernel(**inputs):
    import numpy as np
    import concourse.bacc as bacc
    from concourse import mybir as mb
    from concourse.bass_utils import run_bass_kernel_spmd as run

    i = {k: np.asarray(v) for k, v in inputs.items()}
    fr = i["fside_BxS2_0"]
    arrays = {
        "x": i["x"].reshape(4096, 256),
        "ctxT": i["ctx_1024"].reshape(4096, 256).T,
        "frac": fr,
        "fT": fr.reshape(32, 128).T,
        "kT": i["L0_attn_w_fc"].reshape(1024, 64).T,
        "v": i["L0_attn_w_proj"].T.reshape(1024, 64),
        "ln_g": i["L0_attn_ln_g"],
        "ln_b": i["L0_attn_ln_b"],
        "WqT": i["L0_xattn_Wq"].T,
        "WkT": i["L0_xattn_Wk"].T,
        "WvT": i["L0_xattn_Wv"].T,
        "WoT": i["L0_xattn_Wo"].T,
        "bq": i["L0_xattn_bq"].reshape(2, 128).T,
        "bk": i["L0_xattn_bk"].reshape(2, 128).T,
        "bv": i["L0_xattn_bv"].reshape(2, 128).T,
        "bo": i["L0_xattn_bo"],
        "alpha_pos": i["L0_xattn_alpha_pos"],
        "alpha_neg": i["L0_xattn_alpha_neg"],
        "gamma": i["L0_xattn_gamma"].reshape(1),
        "delta": i["L0_xattn_delta"].reshape(1),
        "gateT": i["L0_ffn_gate_W"].T,
        "gate_b": i["L0_ffn_gate_b"].reshape(8, 1),
        "wiT": i["L0_ffn_wi_W"].T,
        "wi_b": i["L0_ffn_wi_b"],
        "woT": i["L0_ffn_wo_W"].T,
        "wo_b": i["L0_ffn_wo_b"],
        "loraA": i["L0_ffn_lora_A"].reshape(32, 256).T,
        "loraB": i["L0_ffn_lora_B"].transpose(0, 2, 1).reshape(32, 1024),
    }
    arrays = {k: np.ascontiguousarray(v) for k, v in arrays.items()}
    nc = bacc.Bacc("TRN2", target_bir_lowering=False, num_devices=1)
    aps = {k: nc.dram_tensor(f"in_{k}", v.shape, mb.dt.from_np(v.dtype), kind="ExternalInput").ap()
           for k, v in arrays.items()}
    o = nc.dram_tensor("out_0", (4096, 256), mb.dt.float32, kind="ExternalOutput").ap()
    decoder_layer(nc, aps, o)
    r = run(nc, [{f"in_{k}": v for k, v in arrays.items()}], core_ids=[0])
    return r.results[0]["out_0"].reshape(16, 256, 256)
```
